# Optimizing a Trainium2 kernel written in Bass

```python
import numpy as np
import jax
import jax.numpy as jnp

def _softmax(x, axis=-1):
    return jax.nn.softmax(x, axis=axis)

def _gelu(x):
    return jax.nn.gelu(x, approximate=True)

def _silu(x):
    return jax.nn.silu(x)

def _sigmoid(x):
    return jax.nn.sigmoid(x)

def _layernorm(x, axis=-1, eps=1e-05):
    m = jnp.mean(x, axis=axis, keepdims=True)
    v = jnp.var(x, axis=axis, keepdims=True)
    return (x - m) / jnp.sqrt(v + eps)

def _scatter_add(tgt, idx, src, axis=0):
    return tgt.at[idx].add(src)

def _segment_sum(src, seg, n):
    return jax.ops.segment_sum(src, seg, n)
kernel_name = 'mk_conv_preact_d2_conv_nchw512_r2_f55387'

def setup_inputs(seed: int=0):
    np.random.seed(seed)
    _w = jnp.asarray

    def _rec_inputs():
        import jax
        import jax.numpy as jnp
        _gk = jax.random.key(seed)
        x = -0.000125 + 0.9999 * jax.random.normal(jax.random.fold_in(_gk, 1), (16, 256, 32, 32), jnp.float32)
        return x
    x = _rec_inputs()

    def _L0_conv_setup():
        import jax, jax.numpy as jnp
        from jax import lax
        import numpy as np
        key = jax.random.key(seed)
        ks = jax.random.split(key, 16)
        N, C, H, W = (16, 256, 32, 32)
        Cm, planes, k = (64, 256, 5)
        s = 0.05
        return {'x': jax.random.normal(ks[0], (N, C, H, W), jnp.float32), 'conv_w': jax.random.normal(ks[1], (Cm, C, 1, 1), jnp.float32) * s, 'conv_b': jax.random.normal(ks[2], (Cm,), jnp.float32) * s, 'conv_k_w': jax.random.normal(ks[3], (1, 2, 1, 1), jnp.float32) * s, 'conv_k_b': jax.random.normal(ks[4], (1,), jnp.float32) * s, 'conv_k2_w': jax.random.normal(ks[5], (1, 2, 1, 1), jnp.float32) * s, 'conv_k2_b': jax.random.normal(ks[6], (1,), jnp.float32) * s, 'conv_kernel_w': jax.random.normal(ks[7], (k * k, 1, 1, 1), jnp.float32) * s, 'conv_kernel_b': jax.random.normal(ks[8], (k * k,), jnp.float32) * s, 'conv_kernel2_w': jax.random.normal(ks[9], (9, 1, 1, 1), jnp.float32) * s, 'conv_kernel2_b': jax.random.normal(ks[10], (9,), jnp.float32) * s, 'adap_bias': jax.random.normal(ks[11], (Cm,), jnp.float32) * s, 'atrous_bias': jax.random.normal(ks[12], (Cm,), jnp.float32) * s, 'fuse_w': jax.random.normal(ks[13], (planes, 2 * Cm, 1, 1), jnp.float32) * s, 'fuse_b': jax.random.normal(ks[14], (planes,), jnp.float32) * s}
    _L0_conv_all = _L0_conv_setup()
    _L0_conv_in = {k: v for k, v in _L0_conv_all.items() if k in ('conv_w', 'conv_b', 'conv_k_w', 'conv_k_b', 'conv_k2_w', 'conv_k2_b', 'conv_kernel_w', 'conv_kernel_b', 'conv_kernel2_w', 'conv_kernel2_b', 'adap_bias', 'atrous_bias', 'fuse_w', 'fuse_b')}
    del _L0_conv_all

    def _L1_conv_setup():
        import jax, jax.numpy as jnp
        import numpy as np
        BLOCK = 8
        HALO = 4
        HEADS = 16
        DIM = 256

        def rel_to_abs(x):
            b, l, m = x.shape
            r = (m + 1) // 2
            x = jnp.pad(x, ((0, 0), (0, 0), (0, 1)))
            flat = x.reshape(b, l * (m + 1))
            flat = jnp.pad(flat, ((0, 0), (0, m - l)))
            return flat.reshape(b, l + 1, m)[:, :l, m - r:]

        def relative_logits_1d(q, rel_k):
            b, H, W, _ = q.shape
            r = (rel_k.shape[0] + 1) // 2
            logits = jnp.einsum('bxyd,rd->bxyr', q, rel_k)
            logits = rel_to_abs(logits.reshape(b * H, W, 2 * r - 1)).reshape(b, H, W, r)
            return jnp.broadcast_to(logits[:, :, None], (b, H, r, W, r))

        def rel_pos_emb(q, rel_h, rel_w, block):
            B, n, d = q.shape
            r = (rel_w.shape[0] + 1) // 2
            qb = q.reshape(B, block, block, d)
            wl = relative_logits_1d(qb, rel_w)
            wl = wl.transpose(0, 1, 3, 2, 4).reshape(B, block * block, r * r)
            hl = relative_logits_1d(qb.transpose(0, 2, 1, 3), rel_h)
            hl = hl.transpose(0, 3, 1, 4, 2).reshape(B, block * block, r * r)
            return wl + hl

        def halo_forward(x, Wq, Wkv, Wout_w, Wout_b, rel_h, rel_w):
            b, c, h, w = x.shape
            block, halo, heads = (BLOCK, HALO, HEADS)
            dh = c // heads
            scale = dh ** (-0.5)
            K = block + 2 * halo
            nbh, nbw = (h // block, w // block)
            nb = nbh * nbw
            q_inp = x.reshape(b, c, nbh, block, nbw, block).transpose(0, 2, 4, 3, 5, 1)
            q_inp = q_inp.reshape(b * nb, block * block, c)
            xp = jnp.pad(x, ((0, 0), (0, 0), (halo, halo), (halo, halo)))
            rows = (jnp.arange(nbh) * block)[:, None] + jnp.arange(K)[None, :]
            cols = (jnp.arange(nbw) * block)[:, None] + jnp.arange(K)[None, :]
            patches = xp[:, :, rows[:, None, :, None], cols[None, :, None, :]]
            kv_inp = patches.transpose(0, 2, 3, 4, 5, 1).reshape(b * nb, K * K, c)
            q = q_inp @ Wq.T
            kv = kv_inp @ Wkv.T
            k, v = jnp.split(kv, 2, axis=-1)

            def split_heads(t):
                B, n, _ = t.shape
                return t.reshape(B, n, heads, dh).transpose(0, 2, 1, 3).reshape(B * heads, n, dh)
            q = split_heads(q) * scale
            k = split_heads(k)
            v = split_heads(v)
            sim = jnp.einsum('bid,bjd->bij', q, k)
            sim = sim + rel_pos_emb(q, rel_h, rel_w, block)
            onesp = jnp.pad(jnp.ones((h, w), x.dtype), ((halo, halo), (halo, halo)))
            mpatch = onesp[rows[:, None, :, None], cols[None, :, None, :]]
            mpatch = mpatch.reshape(nb, K * K) > 0
            mask = jnp.broadcast_to(mpatch[None, :, None, None, :], (b, nb, heads, 1, K * K))
            mask = mask.reshape(b * nb * heads, 1, K * K)
            neg = -jnp.finfo(sim.dtype).max
            sim = jnp.where(mask, neg, sim)
            attn = jax.nn.softmax(sim, axis=-1)
            out = jnp.einsum('bij,bjd->bid', attn, v)
            out = out.reshape(b * nb, heads, block * block, dh).transpose(0, 2, 1, 3)
            out = out.reshape(b * nb, block * block, c)
            out = out @ Wout_w.T + Wout_b
            out = out.reshape(b, nbh, nbw, block, block, c).transpose(0, 5, 1, 3, 2, 4)
            return out.reshape(b, c, h, w)
        key = jax.random.key(seed)
        ks = jax.random.split(key, 7)
        dh = DIM // HEADS
        rel_scale = dh ** (-0.5)
        rel_size = BLOCK + 2 * HALO
        return {'x': jax.random.normal(ks[0], (8, DIM, 40, 40), jnp.float32), 'Wq': jax.random.normal(ks[1], (DIM, DIM), jnp.float32) * 0.02, 'Wkv': jax.random.normal(ks[2], (2 * DIM, DIM), jnp.float32) * 0.02, 'Wout_w': jax.random.normal(ks[3], (DIM, DIM), jnp.float32) * 0.02, 'Wout_b': jnp.zeros((DIM,), jnp.float32), 'rel_h': jax.random.normal(ks[4], (2 * rel_size - 1, dh), jnp.float32) * rel_scale, 'rel_w': jax.random.normal(ks[5], (2 * rel_size - 1, dh), jnp.float32) * rel_scale}
    _L1_conv_all = _L1_conv_setup()
    _L1_conv_in = {k: v for k, v in _L1_conv_all.items() if k in ('Wq', 'Wkv', 'Wout_w', 'Wout_b', 'rel_h', 'rel_w')}
    del _L1_conv_all
    return {'x': x, 'L0_conv_conv_w': _L0_conv_in['conv_w'], 'L0_conv_conv_b': _L0_conv_in['conv_b'], 'L0_conv_conv_k_w': _L0_conv_in['conv_k_w'], 'L0_conv_conv_k_b': _L0_conv_in['conv_k_b'], 'L0_conv_conv_k2_w': _L0_conv_in['conv_k2_w'], 'L0_conv_conv_k2_b': _L0_conv_in['conv_k2_b'], 'L0_conv_conv_kernel_w': _L0_conv_in['conv_kernel_w'], 'L0_conv_conv_kernel_b': _L0_conv_in['conv_kernel_b'], 'L0_conv_conv_kernel2_w': _L0_conv_in['conv_kernel2_w'], 'L0_conv_conv_kernel2_b': _L0_conv_in['conv_kernel2_b'], 'L0_conv_adap_bias': _L0_conv_in['adap_bias'], 'L0_conv_atrous_bias': _L0_conv_in['atrous_bias'], 'L0_conv_fuse_w': _L0_conv_in['fuse_w'], 'L0_conv_fuse_b': _L0_conv_in['fuse_b'], 'L1_conv_Wq': _L1_conv_in['Wq'], 'L1_conv_Wkv': _L1_conv_in['Wkv'], 'L1_conv_Wout_w': _L1_conv_in['Wout_w'], 'L1_conv_Wout_b': _L1_conv_in['Wout_b'], 'L1_conv_rel_h': _L1_conv_in['rel_h'], 'L1_conv_rel_w': _L1_conv_in['rel_w']}

def reference(x, L0_conv_conv_w, L0_conv_conv_b, L0_conv_conv_k_w, L0_conv_conv_k_b, L0_conv_conv_k2_w, L0_conv_conv_k2_b, L0_conv_conv_kernel_w, L0_conv_conv_kernel_b, L0_conv_conv_kernel2_w, L0_conv_conv_kernel2_b, L0_conv_adap_bias, L0_conv_atrous_bias, L0_conv_fuse_w, L0_conv_fuse_b, L1_conv_Wq, L1_conv_Wkv, L1_conv_Wout_w, L1_conv_Wout_b, L1_conv_rel_h, L1_conv_rel_w):
    import jax
    import jax.numpy as jnp

    def _L0_conv_ref(x, conv_w, conv_b, conv_k_w, conv_k_b, conv_k2_w, conv_k2_b, conv_kernel_w, conv_kernel_b, conv_kernel2_w, conv_kernel2_b, adap_bias, atrous_bias, fuse_w, fuse_b):
        import jax, jax.numpy as jnp
        from jax import lax
        import numpy as np
        N, C, H, W = x.shape
        Cm = conv_w.shape[0]
        kk = conv_kernel_w.shape[0]
        k = int(round(kk ** 0.5))
        pad = (k - 1) // 2
        cw = conv_w[:, :, 0, 0]
        f = jax.nn.relu(jnp.einsum('nchw,oc->nohw', x, cw) + conv_b[None, :, None, None])
        g = jax.nn.relu(jnp.einsum('nc,oc->no', x.mean((2, 3)), cw) + conv_b)
        wk = conv_kernel_w[:, 0, 0, 0]
        K_img = g[:, :, None] * wk[None, None, :] + conv_kernel_b[None, None, :]
        K_dom = K_img.mean(0)
        gk = jax.nn.relu(conv_k_w[0, 0, 0, 0] * K_img + conv_k_w[0, 1, 0, 0] * K_dom[None] + conv_k_b[0])
        Wd = gk.reshape(N * Cm, 1, k, k)
        wk2 = conv_kernel2_w[:, 0, 0, 0]
        K2_img = g[:, :, None] * wk2[None, None, :] + conv_kernel2_b[None, None, :]
        K2_dom = K2_img.mean(0)
        gk2 = jax.nn.relu(conv_k2_w[0, 0, 0, 0] * K2_img + conv_k2_w[0, 1, 0, 0] * K2_dom[None] + conv_k2_b[0])
        W2 = gk2.reshape(N * Cm, 1, 3, 3)
        fr = f.reshape(1, N * Cm, H, W)
        y1 = lax.conv_general_dilated(fr, Wd, (1, 1), [(pad, pad), (pad, pad)], feature_group_count=N * Cm)
        y1 = y1.reshape(N, Cm, H, W) + adap_bias[None, :, None, None]
        y2 = lax.conv_general_dilated(fr, W2, (1, 1), [(2, 2), (2, 2)], rhs_dilation=(2, 2), feature_group_count=N * Cm)
        y2 = y2.reshape(N, Cm, H, W) + atrous_bias[None, :, None, None]
        y = jnp.concatenate([y1, y2], axis=1)
        out = jnp.einsum('nchw,oc->nohw', y, fuse_w[:, :, 0, 0]) + fuse_b[None, :, None, None]
        return out

    def _L1_conv_ref(x, Wq, Wkv, Wout_w, Wout_b, rel_h, rel_w):
        import jax, jax.numpy as jnp
        import numpy as np
        BLOCK = 8
        HALO = 4
        HEADS = 16
        DIM = 256

        def rel_to_abs(x):
            b, l, m = x.shape
            r = (m + 1) // 2
            x = jnp.pad(x, ((0, 0), (0, 0), (0, 1)))
            flat = x.reshape(b, l * (m + 1))
            flat = jnp.pad(flat, ((0, 0), (0, m - l)))
            return flat.reshape(b, l + 1, m)[:, :l, m - r:]

        def relative_logits_1d(q, rel_k):
            b, H, W, _ = q.shape
            r = (rel_k.shape[0] + 1) // 2
            logits = jnp.einsum('bxyd,rd->bxyr', q, rel_k)
            logits = rel_to_abs(logits.reshape(b * H, W, 2 * r - 1)).reshape(b, H, W, r)
            return jnp.broadcast_to(logits[:, :, None], (b, H, r, W, r))

        def rel_pos_emb(q, rel_h, rel_w, block):
            B, n, d = q.shape
            r = (rel_w.shape[0] + 1) // 2
            qb = q.reshape(B, block, block, d)
            wl = relative_logits_1d(qb, rel_w)
            wl = wl.transpose(0, 1, 3, 2, 4).reshape(B, block * block, r * r)
            hl = relative_logits_1d(qb.transpose(0, 2, 1, 3), rel_h)
            hl = hl.transpose(0, 3, 1, 4, 2).reshape(B, block * block, r * r)
            return wl + hl

        def halo_forward(x, Wq, Wkv, Wout_w, Wout_b, rel_h, rel_w):
            b, c, h, w = x.shape
            block, halo, heads = (BLOCK, HALO, HEADS)
            dh = c // heads
            scale = dh ** (-0.5)
            K = block + 2 * halo
            nbh, nbw = (h // block, w // block)
            nb = nbh * nbw
            q_inp = x.reshape(b, c, nbh, block, nbw, block).transpose(0, 2, 4, 3, 5, 1)
            q_inp = q_inp.reshape(b * nb, block * block, c)
            xp = jnp.pad(x, ((0, 0), (0, 0), (halo, halo), (halo, halo)))
            rows = (jnp.arange(nbh) * block)[:, None] + jnp.arange(K)[None, :]
            cols = (jnp.arange(nbw) * block)[:, None] + jnp.arange(K)[None, :]
            patches = xp[:, :, rows[:, None, :, None], cols[None, :, None, :]]
            kv_inp = patches.transpose(0, 2, 3, 4, 5, 1).reshape(b * nb, K * K, c)
            q = q_inp @ Wq.T
            kv = kv_inp @ Wkv.T
            k, v = jnp.split(kv, 2, axis=-1)

            def split_heads(t):
                B, n, _ = t.shape
                return t.reshape(B, n, heads, dh).transpose(0, 2, 1, 3).reshape(B * heads, n, dh)
            q = split_heads(q) * scale
            k = split_heads(k)
            v = split_heads(v)
            sim = jnp.einsum('bid,bjd->bij', q, k)
            sim = sim + rel_pos_emb(q, rel_h, rel_w, block)
            onesp = jnp.pad(jnp.ones((h, w), x.dtype), ((halo, halo), (halo, halo)))
            mpatch = onesp[rows[:, None, :, None], cols[None, :, None, :]]
            mpatch = mpatch.reshape(nb, K * K) > 0
            mask = jnp.broadcast_to(mpatch[None, :, None, None, :], (b, nb, heads, 1, K * K))
            mask = mask.reshape(b * nb * heads, 1, K * K)
            neg = -jnp.finfo(sim.dtype).max
            sim = jnp.where(mask, neg, sim)
            attn = jax.nn.softmax(sim, axis=-1)
            out = jnp.einsum('bij,bjd->bid', attn, v)
            out = out.reshape(b * nb, heads, block * block, dh).transpose(0, 2, 1, 3)
            out = out.reshape(b * nb, block * block, c)
            out = out @ Wout_w.T + Wout_b
            out = out.reshape(b, nbh, nbw, block, block, c).transpose(0, 5, 1, 3, 2, 4)
            return out.reshape(b, c, h, w)
        return halo_forward(x, Wq, Wkv, Wout_w, Wout_b, rel_h, rel_w)

    def _gn(v, G=32, eps=1e-05):
        B_, C_, H_, W_ = v.shape
        g = v.reshape(B_, G, C_ // G, H_, W_)
        m = jnp.mean(g, axis=(2, 3, 4), keepdims=True)
        s = jnp.var(g, axis=(2, 3, 4), keepdims=True)
        return ((g - m) / jnp.sqrt(s + eps)).reshape(v.shape)

    def _ln_c(v, eps=1e-06):
        m = jnp.mean(v, axis=1, keepdims=True)
        s = jnp.var(v, axis=1, keepdims=True)
        return (v - m) / jnp.sqrt(s + eps)

    def _ln_t(v, eps=1e-05):
        m = jnp.mean(v, axis=-1, keepdims=True)
        s = jnp.var(v, axis=-1, keepdims=True)
        return (v - m) / jnp.sqrt(s + eps)

    def _to_tokens(v):
        B_, C_, H_, W_ = v.shape
        return v.reshape(B_, C_, H_ * W_).transpose(0, 2, 1)

    def _from_tokens(t, like):
        B_, C_, H_, W_ = like.shape
        return t.transpose(0, 2, 1).reshape(B_, C_, H_, W_)
    x = x + _L0_conv_ref(_gn(x), L0_conv_conv_w, L0_conv_conv_b, L0_conv_conv_k_w, L0_conv_conv_k_b, L0_conv_conv_k2_w, L0_conv_conv_k2_b, L0_conv_conv_kernel_w, L0_conv_conv_kernel_b, L0_conv_conv_kernel2_w, L0_conv_conv_kernel2_b, L0_conv_adap_bias, L0_conv_atrous_bias, L0_conv_fuse_w, L0_conv_fuse_b)
    x = x + _L1_conv_ref(_gn(x), L1_conv_Wq, L1_conv_Wkv, L1_conv_Wout_w, L1_conv_Wout_b, L1_conv_rel_h, L1_conv_rel_w)
    return x

_drawn_inputs = setup_inputs


def setup_inputs(seed=0):
    import zlib

    import numpy as np

    out = dict(_drawn_inputs(seed))
    spreads = {'L1_conv_Wout_b': (0.0, 0.1)}
    factors = {'L0_conv_conv_b': 8.0,
     'L0_conv_conv_k2_w': 8.0,
     'L0_conv_conv_kernel2_w': 8.0,
     'L0_conv_conv_kernel2_b': 8.0,
     'L0_conv_adap_bias': 2.872,
     'L0_conv_atrous_bias': 3.274,
     'L1_conv_Wkv': 8.0,
     'L1_conv_Wout_w': 8.0}
    for name, (base, spread) in spreads.items():
        noise = np.random.default_rng([zlib.crc32(name.encode()), seed]).standard_normal(out[name].shape)
        drawn = base * np.exp(spread * noise) if base else spread * noise
        out[name] = jnp.asarray(drawn.astype(out[name].dtype))
    for name, factor in factors.items():
        out[name] = (out[name] * factor).astype(out[name].dtype)
    return out
```

```python
from contextlib import ExitStack

import numpy as np
import concourse.bass as bass
from concourse import mybir

F32 = mybir.dt.float32
F32R = mybir.dt.float32r
BF16 = mybir.dt.bfloat16
ALU = mybir.AluOpType
ACT = mybir.ActivationFunctionType
AX = mybir.AxisListType

N, C, H, W = 16, 256, 32, 32
HW = H * W
HALF = HW // 2
NC2 = C // 128
CM = 64
GROUP = 8
EPS = 1e-5
BATCH = 4
ITERS = N // BATCH
PITCH = W + 2
PAIR = (H + 2) * PITCH
PADDED = (H + 4) * PITCH + 2
SPAN = H * PITCH
N1, N2 = 25, 9
SHARED = [5 * a + b for a in (0, 2, 4) for b in (0, 2, 4)]
ALONE = [t for t in range(N1) if t not in SHARED]
TAPS = ALONE + SHARED
NA = len(ALONE)
OFFSET = [(t // 5) * PITCH + t % 5 for t in TAPS]
PASSES = NA + 2 * N2
CHUNKS = [(0, 4), (4, 4), (8, 4), (12, 4), (16, 5), (21, 5), (26, 4), (30, 4)]
NCH = len(CHUNKS)
UCH = 4
COLUMNS = 128 + CM + 2 * C + 2 + 2 * NC2
START = 1
CHMAX = max(n for _, n in CHUNKS)
WIN = 16
KEYS = WIN * WIN
IN0, IN1 = 8, 24


def tap_of(q):
    return q if q < NA + N2 else q - N2


def build(nc, x, cw_t, taps, columns, wkv, wout_t, out):
    with ExitStack() as ctx:
        def sb(name, shape, dt=F32):
            return ctx.enter_context(nc.sbuf_tensor(name, shape, dt))

        def pb(name):
            return ctx.enter_context(nc.psum_tensor(name, [128, HW], F32))

        def sem(name):
            return ctx.enter_context(nc.semaphore(name))

        xs = sb("xs", [128, N * NC2 * HW])
        fpad = sb("fpad", [128, 7 * PAIR + 4 * PITCH + 4 + SPAN])
        hl = [sb(f"hl{b}", [128, PADDED + 2], F32R) for b in range(2)]
        wdiag = [sb(f"wdiag{b}", [128, CHMAX * 128], F32R) for b in range(2)]
        uv = sb("uv", [128, 2 * HW])
        yd = [sb(f"yd{b}", [128, HW]) for b in range(2)]
        tmp = [sb(f"tmp{b}", [128, HALF]) for b in range(2)]
        junk = sb("junk", [128, HALF], BF16)
        cst = sb("cst", [128, COLUMNS])
        gmat, eye = cst[:, 0:128], cst[:, 128:192]
        fw, fwu = cst[:, 192:448], cst[:, 448:704]
        cb, yb = cst[:, 704:705], cst[:, 705:706]
        fb = cst[:, 706:708]
        wb = cst[:, 708:710]
        tm = sb("tm", [128, 2 * (N1 + N2) + 6])
        tapv = tm[:, 0:2 * (N1 + N2)]
        mixv = tm[:, 2 * (N1 + N2):]
        nwb = sb("nwb", [128, NC2])
        mv = sb("mv", [128, N, NC2, 2])
        gm = sb("gm", [128, NC2, N])
        gw = sb("gw", [128, 2 * BATCH * PASSES * 2])
        gd = sb("gd", [128, ITERS * (N1 + N2)])
        gdi = sb("gdi", [128, N1 + N2])
        acc_s = sb("acc_s", [128, N * NC2 * 2])
        acc_q = sb("acc_q", [128, N * NC2 * 2])
        acc_w = sb("acc_w", [128, N * NC2 * 4])
        sm = sb("sm", [128, 24])
        cw = uv[:, 0:256].rearrange("p (c m) -> p c m", c=NC2)
        wsc = [uv[:, 512 + 512 * b:1024 + 512 * b].rearrange("p (c j m) -> p c j m", c=NC2, j=BATCH)
               for b in range(2)]
        bst = uv[:, 1536:1536 + 24 * BATCH].rearrange("p (j c h s) -> p j c h s", j=BATCH, c=NC2, h=2)
        gin = yd[0][:, 0:16].rearrange("p (j c s) -> p j c s", j=BATCH, c=NC2)
        gout = yd[0][:, 16:32].rearrange("p (j c s) -> p j c s", j=BATCH, c=NC2)
        vareps = yd[0][:, 32:40].rearrange("p (j c) -> p j c", j=BATCH)
        rstd = yd[0][:, 40:48].rearrange("p (j c) -> p j c", j=BATCH)
        gmr = yd[0][:, 48:56].rearrange("p (c j) -> p c j", c=NC2)
        minus_half = sb("minus_half", [128, 2 * N])
        fbias = yd[0][:, 96:104]
        gall = yd[0][:, 128:144]
        gbar = yd[0][:, 144:146]
        s12 = yd[0][:, 160:192].rearrange("p (k n) -> p k n", k=2)
        sd = yd[0][:, 192:200].rearrange("p (k i) -> p k i", k=2)
        dt = yd[0][:, 200:234]
        gk = yd[1][:, 0:8 * 34].rearrange("p (n t) -> p n t", n=8)
        gkh = yd[1][:, 512:512 + 8 * 34].rearrange("p (n t) -> p n t", n=8)

        pu, pv, pf, pd = pb("pu"), pb("pv"), pb("pf"), pb("pd")

        s_const = sem("const_loaded")
        s_cw = sem("conv_w_loaded")
        s_x = [sem(f"x_loaded{n}") for n in range(N)]
        s_dve = sem("dve_step")
        s_pool = sem("pool_step")
        s_zero = sem("pads_zeroed")
        s_gin = sem("channel_stats_ready")
        s_gout = sem("group_stats_done")
        s_var = sem("variance_ready")
        s_rstd = sem("rstd_ready")
        s_gmr = sem("shift_ready")
        s_pbias = sem("shift_product_done")
        s_wsc = sem("scaled_weights_ready")
        s_fbias = sem("f_bias_ready")
        s_fmm = sem("f_products_done")
        s_fev = sem("f_stored")
        s_gmm = sem("g_product_done")
        s_s12 = sem("kernel_scales_ready")
        s_gw = sem("kernel_values_ready")
        s_gm = sem("pixel_means_ready")
        s_hi = sem("hi_parts_ready")
        s_hl = sem("hi_lo_ready")
        s_diag = sem("diagonals_ready")
        s_pass = sem("chunk_passed")
        s_uev, s_vev = sem("u_stored"), sem("v_stored")
        s_yd = sem("d_sums_ready")
        s_fuse = sem("fuse_half_done")
        s_tmp = sem("fused_half_in_tmp")
        s_add = sem("x1_half_ready")
        s_stat = sem("x1_statistic_done")
        s_attw = sem("attention_weights_loaded")
        s_t = sem("tail_product_done")
        s_tv = sem("tail_operand_ready")
        s_tp = sem("tail_rstd_ready")
        s_inner = sem("inner_blocks_added")
        s_store = sem("stored")

        def xh(n, c, h):
            return xs[:, bass.ds((n * NC2 + c) * HW + h * HALF, HALF)]

        def shifted(tile, base, off, parts=slice(0, 128), rows=slice(0, H)):
            full = tile[parts, bass.ds(base + off + rows.start * PITCH, (rows.stop - rows.start) * PITCH)]
            return full.rearrange("p (r c) -> p r c", c=PITCH)[:, :, 0:W]

        def image(ap):
            return ap.rearrange("p (r c) -> p r c", c=W)

        INTERIOR = 2 * PITCH + 2
        LO, HI = slice(0, 64), slice(64, 128)

        x_v = x.rearrange("n (c p) h w -> p (n c) (h w)", p=128)
        out_v = out.rearrange("n (c p) h w -> p (n c) (h w)", p=128)

        block = ctx.enter_context(nc.Block())

        @block.sync
        def _(sp):
            for n in range(N):
                sp.dma_start(xs[:, n * NC2 * HW:(n + 1) * NC2 * HW].rearrange("p (c f) -> p c f", c=NC2),
                             x_v[:, n * NC2:(n + 1) * NC2, :]).then_inc(s_x[n], 16)
            with sp.Fori(0, ITERS) as i:
                for j in (2, 3, 0, 1):
                    done = (2, 3, 0, 1).index(j)
                    sp.wait_ge(s_add, START + (i * BATCH + done + 1) * 4)
                    src = xs[:, bass.ds((i * BATCH + j) * NC2 * HW, NC2 * HW)]
                    src = src.rearrange("p (c f) -> p c f", c=NC2)
                    for r0, r1 in ((0, IN0), (IN1, H)):
                        sp.dma_start(out_v[:, bass.ds((i * BATCH + j) * NC2, NC2), r0 * W:r1 * W],
                                     src[:, :, r0 * W:r1 * W]).then_inc(s_store, 16)
            sp.wait_ge(s_fuse, START + 16 * ITERS)
            sp.dma_start(yd[0][:, 0:512].rearrange("p (k c) -> p k c", k=2),
                         wkv[C:2 * C, :].rearrange("(k p) c -> p k c", p=128)).then_inc(s_attw, 16)
            sp.dma_start(yd[1][:, 0:512].rearrange("p (k o) -> p k o", k=2),
                         wout_t.rearrange("(k p) o -> p k o", p=128)).then_inc(s_attw, 16)
            for n in range(N):
                sp.wait_ge(s_inner, n + 1)
                src = xs[:, n * NC2 * HW:(n + 1) * NC2 * HW].rearrange("p (c f) -> p c f", c=NC2)
                sp.dma_start(out_v[:, n * NC2:(n + 1) * NC2, IN0 * W:IN1 * W], src[:, :, IN0 * W:IN1 * W]).then_inc(s_store, 16)
            sp.wait_ge(s_store, 16 * 3 * N)

        @block.gpsimd
        def _(pool):
            steps = [0]

            def link(ins):
                steps[0] += 1
                ins.then_inc(s_pool, 1)
                pool.wait_ge(s_pool, steps[0])

            pool.sem_inc(s_add, START)
            link(pool.memset(minus_half[:, :], -0.5))
            pool.memset(fpad[:, :], 0.0).then_inc(s_zero, 1)
            for k in range(ITERS):
                pool.wait_ge(s_var, k + 1)
                pool.tensor_tensor(yd[0][:, 40:48], yd[0][:, 32:40], minus_half[:, 0:8], ALU.pow).then_inc(s_rstd, 1)
            pool.wait_ge(s_s12, 4)
            for k in range(2):
                t0, t1 = (0, N1) if k == 0 else (N1, N1 + N2)
                for m in range(2):
                    link(pool.tensor_tensor(
                        gk[:, m::2, t0:t1], tapv[:, t0:t1].unsqueeze(1).to_broadcast([128, ITERS, t1 - t0]),
                        s12[:, k, 2 + m::4].unsqueeze(2).to_broadcast([128, ITERS, t1 - t0]), ALU.mult))
            link(pool.tensor_tensor(gk, gk, dt.unsqueeze(1).to_broadcast([128, 8, N1 + N2]), ALU.add))
            link(pool.tensor_scalar(yd[1][:, 0:272], yd[1][:, 0:272], 0.0, None, ALU.max))
            link(pool.tensor_copy(yd[1][:, 512:784].bitcast(F32R), yd[1][:, 0:272]))
            gw4 = gw[:, :].rearrange("p (n q s) -> p n q s", n=8, s=2)
            for q0, n, s, t0, part in ((0, NA, 0, 0, "hi"), (0, NA, 1, 0, "lo"),
                                       (NA, N2, 0, NA, "hi"), (NA, N2, 1, N1, "hi"),
                                       (NA + N2, N2, 0, NA, "lo"), (NA + N2, N2, 1, N1, "lo")):
                dst = gw4[:, :, q0:q0 + n, s]
                if part == "hi":
                    ins = pool.tensor_copy(dst, gkh[:, :, t0:t0 + n])
                else:
                    ins = pool.tensor_tensor(dst, gk[:, :, t0:t0 + n], gkh[:, :, t0:t0 + n], ALU.subtract)
                ins.then_inc(s_gw, 1)
            pool.wait_ge(s_gw, 6)

            def diagonals(i, m, k, fresh=False):
                j = m * NCH + k
                q0, n = CHUNKS[k]
                if not fresh:
                    pool.wait_ge(s_pass, START + i * (2 * NCH) + (j - 1))
                vals = gw[:, bass.ds((i * 2 + m) * (2 * PASSES) + 2 * q0, 2 * n)]
                pool.tensor_tensor(wdiag[j % 2][:, 0:n * 128].rearrange("p (q m) -> p q m", m=CM),
                                   eye.unsqueeze(1).to_broadcast([128, 2 * n, CM]),
                                   vals.unsqueeze(2).to_broadcast([128, 2 * n, CM]), ALU.mult).then_inc(s_diag, 1)

            def adds(i, s, j):
                for u in range(4):
                    pool.wait_ge(s_tmp, START + i * 16 + (4 * s + u + 1))
                    dst = xh(i * BATCH + j, u // 2, u % 2)
                    pool.tensor_tensor(dst, tmp[u % 2][:, :], dst, ALU.add).then_inc(s_add, 1)

            def iteration(i, last):
                for k in range(2, NCH):
                    diagonals(i, 0, k)
                for k in range(2):
                    diagonals(i, 1, k)
                adds(i, 0, 2)
                for k in range(2, NCH):
                    diagonals(i, 1, k)
                if not last:
                    for k in range(2):
                        diagonals(i + 1, 0, k)
                adds(i, 1, 3)
                adds(i, 2, 0)
                adds(i, 3, 1)

            for k in range(2):
                diagonals(0, 0, k, fresh=True)
            with pool.Fori(0, ITERS - 1) as i:
                iteration(i, False)
            iteration(ITERS - 1, True)
            pool.wait_ge(s_tv, 2)
            pool.tensor_tensor(tmp[0][:, 224:256], tmp[0][:, 192:224], minus_half[:, :], ALU.pow).then_inc(s_tp, 1)

        @block.scalar
        def _(act):
            act.dma_start(cst[:, :], columns).then_inc(s_const, 16)
            act.dma_start(cw, cw_t.rearrange("(c p) m -> p c m", p=128)).then_inc(s_cw, 16)
            act.dma_start(tm[:, :], taps.to_broadcast([128, 2 * (N1 + N2) + 6])).then_inc(s_const, 16)
            act.sem_inc(s_uev, START)
            act.sem_inc(s_vev, START)
            act.sem_inc(s_tmp, START)
            act.wait_ge(s_zero, 1)
            for k in range(ITERS):
                for pr, src in ((k, pu), (ITERS + k, pv)):
                    p = 0 if src is pu else 1
                    act.wait_ge(s_fmm, 2 * k + p + 1)
                    act.wait_ge(s_fbias, 2 * (k + 1))
                    bias = fbias[:, 2 * (k % 2) + p:2 * (k % 2) + p + 1]
                    act.activation(shifted(fpad, pr * PAIR, INTERIOR), image(src[:, :]), ACT.Relu,
                                   bias=bias).then_inc(s_fev, 1)

            def hi_a(i, first=False):
                if not first:
                    act.wait_ge(s_pass, START + i * (2 * NCH) - NCH)
                act.activation(hl[0][LO, 0:PADDED], fpad[LO, bass.ds((i + ITERS) * PAIR, PADDED)],
                               ACT.Copy).then_inc(s_hi, 1)

            def hi_b(i, first=False):
                if not first:
                    act.wait_ge(s_pass, START + i * (2 * NCH))
                for parts in (HI, LO):
                    act.activation(hl[1][parts, 0:PADDED], fpad[HI, bass.ds((i + ITERS) * PAIR, PADDED)],
                                   ACT.Copy).then_inc(s_hi, 1)

            def store_u(i, m):
                act.wait_ge(s_pass, START + i * (2 * NCH) + (m * NCH + UCH))
                act.activation(uv[:, 0:HW], pu[:, :], ACT.Copy).then_inc(s_uev, 1)

            def store_v(i, m):
                act.wait_ge(s_pass, START + i * (2 * NCH) + (m * NCH + NCH))
                act.activation(uv[:, HW:2 * HW], pv[:, :], ACT.Copy).then_inc(s_vev, 1)

            def fused(i, s, j):
                for u in range(4):
                    v = 4 * s + u
                    act.wait_ge(s_fuse, START + i * 16 + (v + 1))
                    act.wait_ge(s_add, START + i * 16 + max(v - 1, 0))
                    col = acc_s[:, bass.ds((i * BATCH + j) * 4 + u, 1)]
                    act.activation(tmp[u % 2][:, :], pf[:, (u % 2) * HALF:(u % 2 + 1) * HALF], ACT.Identity,
                                   bias=fb[:, u // 2:u // 2 + 1], accum_out=col).then_inc(s_tmp, 1)

            def stats(i, s, j):
                act.wait_ge(s_add, START + i * 16 + 4 * (s + 1))
                for u in range(4):
                    act.activation(junk[:, :], xh(i * BATCH + j, u // 2, u % 2), ACT.Square,
                                   bias=nwb[:, u // 2:u // 2 + 1],
                                   accum_out=acc_q[:, bass.ds((i * BATCH + j) * 4 + u, 1)]).then_inc(s_stat, 1)
                    act.wait_ge(s_stat, i * 48 + (12 * s + u + 1))
                for c in range(NC2):
                    img = image(xs[:, bass.ds(((i * BATCH + j) * NC2 + c) * HW, HW)])
                    for w in range(4):
                        r, q = 4 + 8 * (w // 2), 4 + 8 * (w % 2)
                        ins = act.activation(junk[:, 0:KEYS].rearrange("p (r c) -> p r c", c=WIN),
                                             img[:, r:r + WIN, q:q + WIN], ACT.Copy,
                                             accum_out=acc_w[:, bass.ds((i * BATCH + j) * 8 + (4 * c + w), 1)])
                        ins.then_inc(s_stat, 1)
                        act.wait_ge(s_stat, i * 48 + (12 * s + 4 + 4 * c + w + 1))

            def image_a(i):
                store_u(i, 0)
                store_v(i, 0)
                fused(i, 0, 2)

            def iteration(i, last):
                if not last:
                    hi_a(i + 1)
                store_u(i, 1)
                store_v(i, 1)
                fused(i, 1, 3)
                fused(i, 2, 0)
                fused(i, 3, 1)
                stats(i, 0, 2)
                if not last:
                    hi_b(i + 1)
                    image_a(i + 1)
                stats(i, 1, 3)
                stats(i, 2, 0)
                stats(i, 3, 1)

            hi_a(0, first=True)
            hi_b(0, first=True)
            image_a(0)
            with act.Fori(0, ITERS - 1) as i:
                iteration(i, False)
            iteration(ITERS - 1, True)

        @block.vector
        def _(dve):
            steps = [0]

            def link(ins):
                steps[0] += 1
                ins.then_inc(s_dve, 1)
                dve.wait_ge(s_dve, steps[0])

            dve.sem_inc(s_yd, START)
            dve.wait_ge(s_const, 32)
            link(dve.tensor_scalar(nwb[:, :], wb, -1.0, None, ALU.mult))
            for b in range(2):
                dve.memset(hl[b][:, :].bitcast(F32), 0.0)

            def group_sums(k):
                m = mv[:, k * BATCH:(k + 1) * BATCH, :, :]
                link(dve.tensor_tensor(gin[:, :, :, 1], m[:, :, :, 0], m[:, :, :, 0], ALU.mult))
                link(dve.tensor_tensor(gin[:, :, :, 1], gin[:, :, :, 1], m[:, :, :, 1], ALU.add))
                dve.tensor_copy(gin[:, :, :, 0], m[:, :, :, 0]).then_inc(s_gin, 1)

            def variance(k):
                dve.wait_ge(s_gout, k + 1)
                link(dve.tensor_copy(yd[0][:, 16:32], pf[:, 0:16]))
                link(dve.tensor_tensor(vareps, gout[:, :, :, 0], gout[:, :, :, 0], ALU.mult))
                link(dve.tensor_tensor(vareps, gout[:, :, :, 1], vareps, ALU.subtract))
                dve.tensor_scalar(vareps, vareps, EPS, None, ALU.add).then_inc(s_var, 1)

            def scale(k):
                dve.wait_ge(s_rstd, k + 1)
                dve.wait_ge(s_cw, 16)
                dve.tensor_tensor(gmr.rearrange("p c j -> p j c"), gout[:, :, :, 0], rstd, ALU.mult).then_inc(s_gmr, 1)
                if k >= 2:
                    dve.wait_ge(s_fmm, 2 * (k - 1))
                dve.tensor_tensor(wsc[k % 2], cw[:, :, 0:CM].unsqueeze(2).to_broadcast([128, NC2, BATCH, CM]),
                                  rstd.rearrange("p j c -> p c j").unsqueeze(3).to_broadcast([128, NC2, BATCH, CM]),
                                  ALU.mult).then_inc(s_wsc, 1)
                g = gm[:, :, k * BATCH:(k + 1) * BATCH]
                m = mv[:, k * BATCH:(k + 1) * BATCH, :, 0].rearrange("p j c -> p c j")
                link(dve.tensor_tensor(g, m, rstd.rearrange("p j c -> p c j"), ALU.mult))
                dve.tensor_tensor(g, g, gmr, ALU.subtract).then_inc(s_gm, 1)

            def f_bias(k):
                dve.wait_ge(s_pbias, k + 1)
                if k >= 2:
                    dve.wait_ge(s_fev, 2 * (k - 1))
                f = fbias[:, 2 * (k % 2):2 * (k % 2) + 2]
                for parts, first in ((LO, 0), (HI, 1)):
                    dve.tensor_scalar(f[parts, :], pf[parts, HALF + first:HALF + 4:2], -1.0, cb[parts, :],
                                      ALU.mult, ALU.add).then_inc(s_fbias, 1)

            for k in range(ITERS):
                for j in range(BATCH):
                    n = k * BATCH + j
                    dve.wait_ge(s_x[n], 16)
                    for c in range(NC2):
                        for h in range(2):
                            at = (n * NC2 + c) * HW + h * HALF
                            ins = dve.bn_stats(bst[:, j, c, h, :], xs[:, at:at + HALF])
                    link(ins)
                    for c in range(NC2):
                        ins = dve.bn_aggr(mv[:, n, c, :], bst[:, j, c, :, :].rearrange("p h s -> p (h s)"))
                    link(ins)
                    if k >= 1 and j < 3:
                        (variance, scale, f_bias)[j](k - 1)
                group_sums(k)
            k = ITERS - 1
            variance(k)
            scale(k)
            f_bias(k)

            dve.wait_ge(s_gmm, 1)
            link(dve.tensor_scalar(gall, pd[:, 0:N], cb, 0.0, ALU.add, ALU.max))
            link(dve.reduce_sum(gbar[:, 0:1], gall, AX.X))
            for kk in range(2):
                a, b, c = (mixv[:, 3 * kk + e:3 * kk + e + 1] for e in range(3))
                t0, t1 = (0, N1) if kk == 0 else (N1, N1 + N2)
                base = N1 + N2
                link(dve.tensor_scalar(gbar[:, 1:2], gbar[:, 0:1], 1.0 / N, b, ALU.mult, ALU.mult))
                link(dve.tensor_scalar(s12[:, kk, :], gall, a, gbar[:, 1:2], ALU.mult, ALU.add))
                link(dve.tensor_tensor(sm[:, 0:1], a, b, ALU.add))
                link(dve.tensor_scalar(dt[:, t0:t1], tapv[:, base + t0:base + t1], sm[:, 0:1], c, ALU.mult, ALU.add))
                for parts, first in ((LO, 0), (HI, 1)):
                    dve.tensor_copy(sd[parts, kk, :], s12[parts, kk, first::4]).then_inc(s_s12, 1)
            dve.wait_ge(s_s12, 4)
            gd3 = gd[:, :].rearrange("p (i t) -> p i t", i=ITERS)
            for kk in range(2):
                t0, t1 = (0, N1) if kk == 0 else (N1, N1 + N2)
                link(dve.tensor_tensor(gd3[:, :, t0:t1], tapv[:, t0:t1].unsqueeze(1).to_broadcast([128, ITERS, t1 - t0]),
                                       sd[:, kk, :].unsqueeze(2).to_broadcast([128, ITERS, t1 - t0]), ALU.mult))
            link(dve.tensor_tensor(gd3, gd3, dt.unsqueeze(1).to_broadcast([128, ITERS, N1 + N2]), ALU.add))
            link(dve.tensor_scalar(gd[:, :], gd[:, :], 0.0, None, ALU.max))
            link(dve.tensor_tensor(fb, fb, wb, ALU.add))
            link(dve.tensor_tensor(fb, pd[:, HALF:HALF + NC2], fb, ALU.add))
            base_steps = steps[0]

            def lo_a(i):
                dve.wait_ge(s_hi, i * 3 + 1)
                dve.tensor_tensor(hl[0][HI, 0:PADDED], fpad[LO, bass.ds((i + ITERS) * PAIR, PADDED)],
                                  hl[0][LO, 0:PADDED].bitcast(F32), ALU.subtract).then_inc(s_hl, 1)

            def lo_b(i):
                dve.wait_ge(s_hi, i * 3 + 3)
                dve.tensor_tensor(hl[1][HI, 0:PADDED], fpad[HI, bass.ds((i + ITERS) * PAIR, PADDED)],
                                  hl[1][HI, 0:PADDED].bitcast(F32), ALU.subtract).then_inc(s_hl, 1)

            PER = 1 + NA + 2 * (N2 - 1)

            def iteration(i, last):
                n = [0]

                def chained(ins, back):
                    n[0] += 1
                    ins.then_inc(s_dve, 1)
                    if back is not None:
                        dve.wait_ge(s_dve, i * PER + (base_steps + n[0] - back))

                base = i * PAIR
                dve.wait_ge(s_yd, START + i * 4)
                chained(dve.tensor_copy(gdi[:, :], gd[:, bass.ds(i * (N1 + N2), N1 + N2)]), 0)
                acc1 = image(pd[:, :])
                acc2 = image(yd[1][:, :])

                def tap1(t, parts=slice(0, 128), dst=acc1):
                    f, g = shifted(fpad, base, OFFSET[t], parts), gdi[parts, t:t + 1]
                    if t == 0:
                        return dve.tensor_scalar(dst[parts], f, g, None, ALU.mult)
                    return dve.scalar_tensor_tensor(out=dst, in0=f, scalar=g, in1=acc1[parts],
                                                    op0=ALU.mult, op1=ALU.add)

                def tap2(j, parts=slice(0, 128), dst=acc2):
                    f, g = shifted(fpad, base, OFFSET[NA + j], parts), gdi[parts, N1 + j:N1 + j + 1]
                    if j == 0:
                        return dve.tensor_scalar(dst, f, g, None, ALU.mult)
                    return dve.scalar_tensor_tensor(out=dst, in0=f, scalar=g, in1=acc2[parts],
                                                    op0=ALU.mult, op1=ALU.add)

                for t in range(NA):
                    chained(tap1(t), 0)
                    if t == 10:
                        lo_b(i)
                dve.wait_ge(s_fuse, START + i * 16)
                dve.wait_ge(s_gw, 6)
                for j in range(N2 - 1):
                    chained(tap2(j), 1)
                    chained(tap1(NA + j), 1)
                    if j == 5 and not last:
                        lo_a(i + 1)
                assert n[0] == PER
                dve.wait_ge(s_dve, i * PER + (base_steps + PER))
                tap2(N2 - 1, LO, image(yd[0][HI, :])).then_inc(s_yd, 1)
                tap2(N2 - 1, HI, image(yd[1][HI, :])).then_inc(s_yd, 1)
                tap1(N1 - 1, LO, image(yd[0][LO, :])).then_inc(s_yd, 1)
                dve.wait_ge(s_yd, START + i * 4 + 1)
                tap1(N1 - 1, HI, image(yd[1][LO, :])).then_inc(s_yd, 1)

            dve.wait_ge(s_fev, 2 * ITERS)
            lo_a(0)
            with dve.Fori(0, ITERS - 1) as i:
                iteration(i, False)
            iteration(ITERS - 1, True)

            steps[0] = base_steps + ITERS * PER
            t = tmp[0]
            dve.wait_ge(s_stat, 48 * ITERS)
            gin2 = t[:, 0:64].rearrange("p (n c s) -> p n c s", n=N, c=NC2)
            s3 = acc_s[:, :].rearrange("p (n c h) -> p n c h", n=N, c=NC2)
            q3 = acc_q[:, :].rearrange("p (n c h) -> p n c h", n=N, c=NC2)
            wb3 = wb.unsqueeze(1).to_broadcast([128, N, NC2])
            for e, a in ((0, s3), (1, q3)):
                link(dve.tensor_tensor(gin2[:, :, :, e], a[:, :, :, 0], a[:, :, :, 1], ALU.add))
            link(dve.tensor_scalar(t[:, 0:64], t[:, 0:64], 1.0 / HW, None, ALU.mult))
            link(dve.tensor_tensor(gin2[:, :, :, 0], gin2[:, :, :, 0], mv[:, :, :, 0], ALU.add))
            dve.tensor_tensor(gin2[:, :, :, 0], gin2[:, :, :, 0], wb3, ALU.subtract).then_inc(s_tv, 1)
            dve.wait_ge(s_t, 1)
            link(dve.tensor_copy(t[:, 64:128], pf[:, 0:64]))
            go = t[:, 64:128].rearrange("p (n c s) -> p n c s", n=N, c=NC2)
            ve = t[:, 192:224].rearrange("p (n c) -> p n c", n=N)
            rs = t[:, 224:256].rearrange("p (n c) -> p n c", n=N)
            link(dve.tensor_tensor(ve, go[:, :, :, 0], go[:, :, :, 0], ALU.mult))
            link(dve.tensor_tensor(ve, go[:, :, :, 1], ve, ALU.subtract))
            dve.tensor_scalar(ve, ve, EPS, None, ALU.add).then_inc(s_tv, 1)
            w3 = acc_w[:, :].rearrange("p (n c w) -> p n c w", n=N, c=NC2)
            w2 = acc_w[:, :].rearrange("p (n w) -> p n w", w=4)
            off = t[:, 256:288]
            link(dve.tensor_tensor(off.rearrange("p (n c) -> p n c", n=N), go[:, :, :, 0], wb3, ALU.add))
            link(dve.tensor_scalar(acc_w[:, :], acc_w[:, :], 1.0 / KEYS, None, ALU.mult))
            link(dve.tensor_tensor(w2, w2, off.unsqueeze(2).to_broadcast([128, 2 * N, 4]), ALU.subtract))
            dve.wait_ge(s_tp, 1)
            dve.tensor_tensor(tmp[1][:, 0:128].rearrange("p (c n w) -> p n c w", c=NC2, n=N), w3,
                              rs.unsqueeze(3).to_broadcast([128, N, NC2, 4]), ALU.mult).then_inc(s_tv, 1)
            dve.wait_ge(s_t, 2)
            dve.tensor_copy(uv[:, 0:512], pd[:, 0:512]).then_inc(s_tv, 1)
            dve.wait_ge(s_t, 3)
            link(dve.tensor_copy(tmp[1][:, 128:256], pf[:, 0:128]))
            vec = tmp[1][:, 128:256].rearrange("p (c n w) -> p c n w", c=NC2, n=N)
            for n in range(N):
                for c in range(NC2):
                    img = image(xs[:, (n * NC2 + c) * HW:(n * NC2 + c + 1) * HW])
                    for b in range(2):
                        rows = img[:, IN0 + 8 * b:IN0 + 8 * b + 8, IN0:IN1].rearrange("p r (b c) -> p r b c", b=2)
                        add = vec[:, c, n, 2 * b:2 * b + 2].unsqueeze(1).unsqueeze(3).to_broadcast([128, 8, 2, 8])
                        ins = dve.tensor_tensor(rows, rows, add, ALU.add)
                ins.then_inc(s_inner, 1)

        @block.tensor
        def _(pe):
            pe.sem_inc(s_pass, START)
            pe.sem_inc(s_fuse, START)
            pe.wait_ge(s_const, 32)
            pe.wait_ge(s_cw, 16)

            def groups(k):
                pe.wait_ge(s_gin, k + 1)
                pe.matmul(pf[:, 0:16], gmat, yd[0][:, 0:16], start=True, stop=True).then_inc(s_gout, 1)

            def f_batch(k):
                pe.wait_ge(s_gmr, k + 1)
                for c in range(NC2):
                    mm = pe.matmul(pf[:, HALF:HALF + 4], cw[:, c, :], gmr[:, c, :], start=(c == 0), stop=(c == NC2 - 1))
                mm.then_inc(s_pbias, 1)
                if k == ITERS - 1:
                    pe.wait_ge(s_gm, ITERS)
                    for c in range(NC2):
                        pe.matmul(pd[:, 0:N], cw[:, c, :], gm[:, c, :], start=(c == 0), stop=(c == NC2 - 1))
                    for c in range(NC2):
                        mm = pe.matmul(pd[:, HALF + c:HALF + c + 1], fw[:, 128 * c:128 * (c + 1)], yb,
                                       start=True, stop=True)
                    mm.then_inc(s_gmm, 1)
                pe.wait_ge(s_wsc, k + 1)
                for p, dst in enumerate((pu, pv)):
                    if k >= 1:
                        pe.wait_ge(s_fev, 2 * (k - 1) + p + 1)
                    for h in range(2):
                        for c in range(NC2):
                            for m, parts in enumerate((LO, HI)):
                                j = 2 * p + m
                                at = ((k * BATCH + j) * NC2 + c) * HW + h * HALF
                                mm = pe.matmul(dst[parts, h * HALF:(h + 1) * HALF], wsc[k % 2][:, c, j, :],
                                               xs[:, at:at + HALF], start=(c == 0), stop=(c == NC2 - 1))
                    mm.then_inc(s_fmm, 1)

            for k in range(ITERS):
                groups(k)
                f_batch(k)

            def passes(i, m):
                pe.wait_ge(s_hl, i * 2 + (m + 1))
                for k, (q0, n) in enumerate(CHUNKS):
                    j = m * NCH + k
                    pe.wait_ge(s_diag, i * (2 * NCH) + (j + 1))
                    if q0 == 0:
                        pe.wait_ge(s_uev, START + i * 2 + m)
                    if q0 == NA:
                        pe.wait_ge(s_vev, START + i * 2 + m)
                    dst = pu if q0 < NA else pv
                    for q in range(q0, q0 + n):
                        lhs = wdiag[j % 2][:, (q - q0) * 128:(q - q0 + 1) * 128]
                        for h in range(2):
                            rhs = shifted(hl[m], 0, OFFSET[tap_of(q)], rows=slice(16 * h, 16 * h + 16))
                            mm = pe.matmul(dst[:, h * HALF:(h + 1) * HALF], lhs, rhs,
                                           start=(q in (0, NA)), stop=(q in (NA - 1, PASSES - 1)))
                    mm.then_inc(s_pass, 1)

            def fuse(i, s, operands):
                for u in range(4):
                    pe.wait_ge(s_tmp, START + i * 16 + max(4 * s + u - 1, 0))
                    c, h = u // 2, u % 2
                    for e, (wt, y) in enumerate(operands):
                        mm = pe.matmul(pf[:, h * HALF:(h + 1) * HALF], wt[:, 128 * c:128 * (c + 1)],
                                       y[:, h * HALF:(h + 1) * HALF], start=(e == 0), stop=(e == len(operands) - 1))
                    mm.then_inc(s_fuse, 1)

            with pe.Fori(0, ITERS) as i:
                for m in range(2):
                    passes(i, m)
                    pe.wait_ge(s_uev, START + i * 2 + (m + 1))
                    pe.wait_ge(s_vev, START + i * 2 + (m + 1))
                    fuse(i, m, ((fwu, uv[:, 0:HW]), (fw, uv[:, HW:2 * HW])))
                pe.wait_ge(s_yd, START + i * 4 + 4)
                for m in range(2):
                    fuse(i, 2 + m, ((fw, yd[m]),))

            pe.wait_ge(s_tv, 1)
            pe.matmul(pf[:, 0:4 * N], gmat, tmp[0][:, 0:4 * N], start=True, stop=True).then_inc(s_t, 1)
            pe.wait_ge(s_attw, 32)
            for c in range(NC2):
                for k in range(NC2):
                    mm = pe.matmul(pd[:, 256 * c:256 * (c + 1)], yd[0][:, 256 * k + 128 * c:256 * k + 128 * (c + 1)],
                                   yd[1][:, 256 * k:256 * (k + 1)], start=(k == 0), stop=(k == NC2 - 1))
            mm.then_inc(s_t, 1)
            pe.wait_ge(s_tv, 4)
            for o in range(NC2):
                for c in range(NC2):
                    mm = pe.matmul(pf[:, 64 * o:64 * (o + 1)], uv[:, 256 * c + 128 * o:256 * c + 128 * (o + 1)],
                                   tmp[1][:, 64 * c:64 * (c + 1)], start=(c == 0), stop=(c == NC2 - 1))
            mm.then_inc(s_t, 1)


def kernel(**inputs):
    import concourse.bacc as bacc
    from concourse.bass_utils import run_bass_kernel_spmd as run

    a = {k: np.ascontiguousarray(v) for k, v in inputs.items()}
    k1, k2 = a["L0_conv_conv_kernel_w"].reshape(-1)[TAPS], a["L0_conv_conv_kernel2_w"].reshape(-1)
    b1, b2 = a["L0_conv_conv_kernel_b"][TAPS], a["L0_conv_conv_kernel2_b"]
    channel = np.arange(128)
    group_mean = (channel[:, None] // GROUP == channel[None, :] // GROUP).astype(np.float32) / GROUP
    ident = (channel[:, None] % CM == np.arange(CM)[None, :]).astype(np.float32)
    cw_t = a["L0_conv_conv_w"].reshape(CM, C).T
    fw_t = a["L0_conv_fuse_w"].reshape(C, 2 * CM).T
    conv_b = a["L0_conv_conv_b"].reshape(CM, 1)
    y_bias = np.concatenate([a["L0_conv_adap_bias"], a["L0_conv_atrous_bias"]]).reshape(2 * CM, 1)
    fuse_b = a["L0_conv_fuse_b"].reshape(NC2, 128).T
    wout_b = a["L1_conv_Wout_b"].reshape(NC2, 128).T
    arrays = {
        "x": a["x"],
        "cw_t": np.concatenate([cw_t, cw_t], 1),
        "taps": np.concatenate([k1, k2, b1, b2, a["L0_conv_conv_k_w"].reshape(-1), a["L0_conv_conv_k_b"],
                                a["L0_conv_conv_k2_w"].reshape(-1), a["L0_conv_conv_k2_b"]]).reshape(1, -1),
        "columns": np.concatenate([group_mean, ident, fw_t, np.concatenate([fw_t[:CM], fw_t[:CM]], 0),
                                   np.concatenate([conv_b, conv_b], 0), y_bias, fuse_b, wout_b], 1),
        "wkv": a["L1_conv_Wkv"],
        "wout_t": a["L1_conv_Wout_w"].T,
    }
    arrays = {k + "_dram": np.ascontiguousarray(v) for k, v in arrays.items()}
    nc = bacc.Bacc("TRN2", target_bir_lowering=False, num_devices=1)
    args = [nc.dram_tensor(k, v.shape, mybir.dt.from_np(v.dtype), kind="ExternalInput").ap()
            for k, v in arrays.items()]
    out = nc.dram_tensor("out_dram", (N, C, H, W), F32, kind="ExternalOutput").ap()
    build(nc, *args, out)
    return run(nc, [arrays], core_ids=[0]).results[0]["out_dram"]
```

```python
from contextlib import ExitStack

import numpy as np
import concourse.bass as bass
from concourse import mybir

F32 = mybir.dt.float32
F32R = mybir.dt.float32r
BF16 = mybir.dt.bfloat16
ALU = mybir.AluOpType
ACT = mybir.ActivationFunctionType
AX = mybir.AxisListType

N, C, H, W = 16, 256, 32, 32
HW = H * W
HALF = HW // 2
NC2 = C // 128
CM = 64
GROUP = 8
EPS = 1e-5
BATCH = 4
ITERS = N // BATCH
PITCH = W + 2
PAIR = (H + 2) * PITCH
PADDED = (H + 4) * PITCH + 2
SPAN = H * PITCH
N1, N2 = 25, 9
SHARED = [5 * a + b for a in (0, 2, 4) for b in (0, 2, 4)]
ALONE = [t for t in range(N1) if t not in SHARED]
TAPS = ALONE + SHARED
NA = len(ALONE)
OFFSET = [(t // 5) * PITCH + t % 5 for t in TAPS]
PASSES = NA + 2 * N2
CHUNKS = [(q, min(4, PASSES - q)) for q in range(0, PASSES, 4)]
NCH = len(CHUNKS)
UCH = NA // 4
COLUMNS = 128 + CM + 2 * C + 2 + 2 * NC2
PIECES = ((2, 3, 4), (0, 5), (6, 7, 8), (1, 9))
START = 1
CHMAX = max(n for _, n in CHUNKS)
WIN = 16
KEYS = WIN * WIN
IN0, IN1 = 8, 24


def tap_of(q):
    return q if q < NA + N2 else q - N2


def build(nc, x, cw_t, taps, columns, wkv, wout_t, out):
    with ExitStack() as ctx:
        def sb(name, shape, dt=F32):
            return ctx.enter_context(nc.sbuf_tensor(name, shape, dt))

        def pb(name):
            return ctx.enter_context(nc.psum_tensor(name, [128, HW], F32))

        def sem(name):
            return ctx.enter_context(nc.semaphore(name))

        xs = sb("xs", [128, N * NC2 * HW])
        fpad = sb("fpad", [128, 7 * PAIR + 4 * PITCH + 4 + SPAN])
        hl = [sb(f"hl{b}", [128, PADDED + 2], F32R) for b in range(2)]
        wdiag = [sb(f"wdiag{b}", [128, CHMAX * 128], F32R) for b in range(2)]
        uv = sb("uv", [128, 2 * HW])
        yd = [sb(f"yd{b}", [128, HW]) for b in range(2)]
        tmp = [sb(f"tmp{b}", [128, HALF]) for b in range(2)]
        cst = sb("cst", [128, COLUMNS])
        gmat, eye = cst[:, 0:128], cst[:, 128:192]
        fw, fwu = cst[:, 192:448], cst[:, 448:704]
        cb, yb = cst[:, 704:705], cst[:, 705:706]
        fb = cst[:, 706:708]
        wb = cst[:, 708:710]
        tm = sb("tm", [128, 2 * (N1 + N2) + 6])
        tapv = tm[:, 0:2 * (N1 + N2)]
        mixv = tm[:, 2 * (N1 + N2):]
        nwb = sb("nwb", [128, NC2])
        mv = sb("mv", [128, N, NC2, 2])
        gm = sb("gm", [128, NC2, N])
        gw = sb("gw", [128, 2 * BATCH * PASSES * 2])
        gd = sb("gd", [128, ITERS * (N1 + N2)])
        gdi = sb("gdi", [128, N1 + N2])
        accg = sb("accg", [128, N * NC2 * 2])
        acc1 = sb("acc1", [128, N * NC2])
        acc_w = sb("acc_w", [128, N * NC2 * 4])
        mvs = sb("mvs", [128, N * NC2])
        at = sb("at", [128, NC2 * C])
        minus_half = sb("minus_half", [128, NC2 * BATCH])
        eps = sb("eps", [128, 2])
        free_p = 4 * PAIR + 2 * PITCH + 2
        junk = [fpad[:, free_p + 512 * b:free_p + 512 * (b + 1)].bitcast(BF16) for b in range(2)]
        l1 = fpad[:, 2 * PITCH + 2:2 * PITCH + 162]
        go = l1[:, 0:16].rearrange("p (j c e) -> p j c e", j=BATCH, c=NC2)
        l1v = l1[:, 16:24].rearrange("p (j c) -> p j c", j=BATCH)
        l1r = l1[:, 24:32].rearrange("p (j c) -> p j c", j=BATCH)
        off = l1[:, 32:40].rearrange("p (j c) -> p j c", j=BATCH)
        cen = l1[:, 40:72].rearrange("p (j c w) -> p j c w", j=BATCH, c=NC2)
        gnw = l1[:, 72:104].rearrange("p (c j w) -> p c j w", c=NC2, j=BATCH)
        vec = l1[:, 104:136].rearrange("p (c j w) -> p c j w", c=NC2, j=BATCH)
        cw = uv[:, 0:256].rearrange("p (c m) -> p c m", c=NC2)
        wsc = [uv[:, 512 + 512 * b:1024 + 512 * b].rearrange("p (c j m) -> p c j m", c=NC2, j=BATCH)
               for b in range(2)]
        bst = uv[:, 1536:1536 + 24 * BATCH].rearrange("p (j c h s) -> p j c h s", j=BATCH, c=NC2, h=2)
        gin = yd[0][:, 0:16].rearrange("p (j c s) -> p j c s", j=BATCH, c=NC2)
        gout = yd[0][:, 16:32].rearrange("p (j c s) -> p j c s", j=BATCH, c=NC2)
        vareps = yd[0][:, 32:40].rearrange("p (j c) -> p j c", j=BATCH)
        rstd = yd[0][:, 40:48].rearrange("p (j c) -> p j c", j=BATCH)
        gmr = yd[0][:, 48:56].rearrange("p (c j) -> p c j", c=NC2)
        fbias = yd[0][:, 96:104]
        gall = yd[0][:, 128:144]
        gbar = yd[0][:, 144:146]
        sm = yd[0][:, 146:147]
        s12 = yd[0][:, 160:192].rearrange("p (k n) -> p k n", k=2)
        sd = yd[0][:, 192:200].rearrange("p (k i) -> p k i", k=2)
        dt = yd[0][:, 200:234]
        gk = yd[1][:, 0:8 * 34].rearrange("p (n t) -> p n t", n=8)
        wv = yd[1][:, 0:512]
        wot = yd[1][:, 512:1024]
        junkl = [tmp[b][:, :].bitcast(BF16) for b in range(2)]
        gkh = yd[1][:, 512:512 + 8 * 34].rearrange("p (n t) -> p n t", n=8)

        pu, pv, pf, pd = pb("pu"), pb("pv"), pb("pf"), pb("pd")

        s_const = sem("const_loaded")
        s_cw = sem("conv_w_loaded")
        s_x = [sem(f"x_loaded{n}") for n in range(N)]
        s_dve = sem("dve_step")
        s_pool = sem("pool_step")
        s_zero = sem("pads_zeroed")
        s_gin = sem("channel_stats_ready")
        s_gout = sem("group_stats_done")
        s_var = sem("variance_ready")
        s_rstd = sem("rstd_ready")
        s_gmr = sem("shift_ready")
        s_pbias = sem("shift_product_done")
        s_wsc = sem("scaled_weights_ready")
        s_fbias = sem("f_bias_ready")
        s_fmm = sem("f_products_done")
        s_fev = sem("f_stored")
        s_gmm = sem("g_product_done")
        s_s12 = sem("kernel_scales_ready")
        s_gw = sem("kernel_values_ready")
        s_gm = sem("pixel_means_ready")
        s_gd = sem("d_values_ready")
        s_fb = sem("fusion_bias_ready")
        s_hi = [sem("hi_a_ready"), sem("hi_b_ready")]
        s_hl = [sem("hi_lo_a_ready"), sem("hi_lo_b_ready")]
        s_diag = sem("diagonals_ready")
        s_pass = sem("chunk_passed")
        s_uev, s_vev = sem("u_stored"), sem("v_stored")
        s_yd = sem("d_sums_ready")
        s_fuse = sem("fuse_half_done")
        s_tmp = sem("fused_half_in_tmp")
        s_add = sem("x1_half_ready")
        s_stat = sem("x1_statistic_done")
        s_xs = sem("x_sums_ready")
        s_tap0 = sem("first_taps_done")
        s_gdi = sem("pair_values_ready")
        s_attw = sem("attention_weights_loaded")
        s_atm = sem("attention_product_done")
        s_at = sem("attention_matrix_ready")
        s_sums = sem("x1_sums_ready")
        s_l1g = sem("x1_group_stats_done")
        s_l1e = sem("attention_part_stored")
        s_l1 = sem("l1_step")
        s_gnw = sem("window_means_ready")
        s_vec = sem("inner_vectors_done")
        s_inner = sem("inner_blocks_added")
        s_store = sem("stored")

        def xh(n, c, h):
            return xs[:, bass.ds((n * NC2 + c) * HW + h * HALF, HALF)]

        def shifted(tile, base, off, parts=slice(0, 128), rows=slice(0, H)):
            full = tile[parts, bass.ds(base + off + rows.start * PITCH, (rows.stop - rows.start) * PITCH)]
            return full.rearrange("p (r c) -> p r c", c=PITCH)[:, :, 0:W]

        def place(what, i):
            if what == "a":
                return i * 16 - 4 if not isinstance(i, int) or i > 0 else 0
            if what == "D0":
                return i * 16 + 16 if not isinstance(i, int) or i < ITERS - 1 else 4 * N - 4
            return i * 16 + (4 if what == "b" else 8)

        def stats_before(what, i):
            if what == "a":
                return i * 40 - 10 if not isinstance(i, int) or i > 0 else 0
            if what == "D0":
                return i * 40 + 40 if not isinstance(i, int) or i < ITERS - 1 else 10 * N - 10
            return i * 40 + (10 if what == "b" else 20)

        def at_least(n, expr):
            return max(n, expr) if isinstance(expr, int) else expr

        SLOT_OF = {"D0": 0, "D1": 1, "a": 2, "b": 3}

        def image(ap):
            return ap.rearrange("p (r c) -> p r c", c=W)

        INTERIOR = 2 * PITCH + 2
        LO, HI = slice(0, 64), slice(64, 128)

        x_v = x.rearrange("n (c p) h w -> p (n c) (h w)", p=128)
        out_v = out.rearrange("n (c p) h w -> p (n c) (h w)", p=128)

        block = ctx.enter_context(nc.Block())

        @block.sync
        def _(sp):
            for n in range(N):
                sp.dma_start(xs[:, n * NC2 * HW:(n + 1) * NC2 * HW].rearrange("p (c f) -> p c f", c=NC2),
                             x_v[:, n * NC2:(n + 1) * NC2, :]).then_inc(s_x[n], 16)
            sp.dma_start(wv.rearrange("p (k c) -> p k c", k=2),
                         wkv[C:2 * C, :].rearrange("(k p) c -> p k c", p=128)).then_inc(s_attw, 16)
            sp.dma_start(wot.rearrange("p (k o) -> p k o", k=2),
                         wout_t.rearrange("(k p) o -> p k o", p=128)).then_inc(s_attw, 16)

            def store_rows(n, r0, r1):
                src = xs[:, bass.ds(n * NC2 * HW, NC2 * HW)].rearrange("p (c f) -> p c f", c=NC2)
                sp.dma_start(out_v[:, bass.ds(n * NC2, NC2), r0 * W:r1 * W],
                             src[:, :, r0 * W:r1 * W]).then_inc(s_store, 16)

            def outer_rows(what, i):
                sp.wait_ge(s_add, START + place(what, i) + 4)
                store_rows(i * BATCH + SLOT_OF[what], 0, IN0)
                store_rows(i * BATCH + SLOT_OF[what], IN1, H)

            def inner_rows(i):
                for j in range(BATCH):
                    sp.wait_ge(s_inner, START + i * BATCH + (j + 1))
                    store_rows(i * BATCH + j, IN0, IN1)

            def stores(i, first=False):
                outer_rows("a", i)
                if not first:
                    outer_rows("D0", i - 1)
                outer_rows("b", i)
                outer_rows("D1", i)
                if not first:
                    inner_rows(i - 1)

            stores(0, first=True)
            with sp.Fori(1, ITERS - 1) as i:
                stores(i)
            stores(ITERS - 1)
            outer_rows("D0", ITERS - 1)
            inner_rows(ITERS - 1)
            sp.wait_ge(s_store, 16 * 3 * N)

        @block.gpsimd
        def _(pool):
            steps = [0]

            def link(ins):
                steps[0] += 1
                ins.then_inc(s_pool, 1)
                pool.wait_ge(s_pool, steps[0])

            pool.sem_inc(s_add, START)
            link(pool.memset(minus_half[:, :], -0.5))
            link(pool.memset(eps[:, :], EPS))
            pool.memset(fpad[:, :], 0.0).then_inc(s_zero, 1)
            for k in range(ITERS):
                pool.wait_ge(s_var, k + 1)
                pool.tensor_tensor(yd[0][:, 40:48], yd[0][:, 32:40], minus_half[:, :], ALU.pow).then_inc(s_rstd, 1)
            m3 = mvs[:, :].rearrange("p (n c) -> p n c", c=NC2)
            pool.wait_ge(s_gm, ITERS)
            link(pool.tensor_tensor(m3, mv[:, :, :, 0], wb.unsqueeze(1).to_broadcast([128, N, NC2]), ALU.subtract))
            link(pool.tensor_scalar(mvs[:, :], mvs[:, :], float(HW), None, ALU.mult))
            pool.wait_ge(s_s12, 4)
            for k in range(2):
                t0, t1 = (0, N1) if k == 0 else (N1, N1 + N2)
                for m in range(2):
                    link(pool.tensor_tensor(
                        gk[:, m::2, t0:t1], tapv[:, t0:t1].unsqueeze(1).to_broadcast([128, ITERS, t1 - t0]),
                        s12[:, k, 2 + m::4].unsqueeze(2).to_broadcast([128, ITERS, t1 - t0]), ALU.mult))
            link(pool.tensor_tensor(gk, gk, dt.unsqueeze(1).to_broadcast([128, 8, N1 + N2]), ALU.add))
            link(pool.tensor_scalar(yd[1][:, 0:272], yd[1][:, 0:272], 0.0, None, ALU.max))
            link(pool.tensor_copy(yd[1][:, 512:784].bitcast(F32R), yd[1][:, 0:272]))
            gw4 = gw[:, :].rearrange("p (n q s) -> p n q s", n=8, s=2)
            for q0, n, s, t0, part in ((0, NA, 0, 0, "hi"), (0, NA, 1, 0, "lo"),
                                       (NA, N2, 0, NA, "hi"), (NA, N2, 1, N1, "hi"),
                                       (NA + N2, N2, 0, NA, "lo"), (NA + N2, N2, 1, N1, "lo")):
                dst = gw4[:, :, q0:q0 + n, s]
                if part == "hi":
                    ins = pool.tensor_copy(dst, gkh[:, :, t0:t0 + n])
                else:
                    ins = pool.tensor_tensor(dst, gk[:, :, t0:t0 + n], gkh[:, :, t0:t0 + n], ALU.subtract)
                ins.then_inc(s_gw, 1)
            pool.wait_ge(s_gw, 6)

            def diagonals(i, m, k, fresh=False):
                j = m * NCH + k
                q0, n = CHUNKS[k]
                if not fresh:
                    pool.wait_ge(s_pass, START + i * (2 * NCH) + (j - 1))
                vals = gw[:, bass.ds((i * 2 + m) * (2 * PASSES) + 2 * q0, 2 * n)]
                pool.tensor_tensor(wdiag[j % 2][:, 0:n * 128].rearrange("p (q m) -> p q m", m=CM),
                                   eye.unsqueeze(1).to_broadcast([128, 2 * n, CM]),
                                   vals.unsqueeze(2).to_broadcast([128, 2 * n, CM]), ALU.mult).then_inc(s_diag, 1)

            def add(what, i, u):
                pool.wait_ge(s_tmp, START + place(what, i) + (u + 1))
                dst = xh(i * BATCH + SLOT_OF[what], u // 2, u % 2)
                pool.tensor_tensor(dst, tmp[u % 2][:, :], dst, ALU.add).then_inc(s_add, 1)

            def channel_sums(i):
                pool.wait_ge(s_stat, stats_before("D0", i) + 10)
                sums = accg[:, bass.ds(i * 16, 16)].rearrange("p (n e) -> p n e", e=2)[:, :, 0]
                half = acc1[:, bass.ds(i * 8, 8)]
                pool.tensor_tensor(sums, sums, half, ALU.add).then_inc(s_l1, 1)
                pool.wait_ge(s_l1, i * 7 + 1)
                pool.tensor_tensor(sums, sums, mvs[:, bass.ds(i * 8, 8)], ALU.add).then_inc(s_sums, 1)

            def window_means(i):
                pool.wait_ge(s_l1e, START + i * 2 + 1)
                steps = (
                    lambda: pool.tensor_tensor(l1v, go[:, :, :, 0], go[:, :, :, 0], ALU.mult),
                    lambda: pool.tensor_tensor(l1v, go[:, :, :, 1], l1v, ALU.subtract),
                    lambda: pool.tensor_tensor(l1[:, 16:24], l1[:, 16:24], eps[:, 0:1].to_broadcast([128, 8]), ALU.add),
                    lambda: pool.tensor_tensor(l1[:, 24:32], l1[:, 16:24], minus_half[:, :], ALU.pow),
                    lambda: pool.tensor_tensor(off, go[:, :, :, 0], wb.unsqueeze(1).to_broadcast([128, BATCH, NC2]),
                                               ALU.add),
                    lambda: pool.tensor_tensor(
                        l1[:, 40:72].rearrange("p (n w) -> p n w", w=4),
                        acc_w[:, bass.ds(i * 32, 32)].rearrange("p (n w) -> p n w", w=4),
                        l1[:, 32:40].unsqueeze(2).to_broadcast([128, 8, 4]), ALU.subtract))
                for n, step in enumerate(steps):
                    step().then_inc(s_l1, 1)
                    pool.wait_ge(s_l1, i * 7 + (n + 2))
                pool.tensor_tensor(gnw.rearrange("p c j w -> p j c w"), cen,
                                   l1r.unsqueeze(3).to_broadcast([128, BATCH, NC2, 4]), ALU.mult).then_inc(s_gnw, 1)

            def slot(chunks, halves, between=None):
                for u in range(max(len(chunks), 4)):
                    if u < len(chunks):
                        diagonals(*chunks[u])
                    if halves and u < 4:
                        add(*halves, u)
                    if between and u == 1:
                        between()

            def round_(i, first=False, last=False):
                slot([(i, 1, k) for k in range(2, 6)], ("a", i))
                slot([(i, 1, k) for k in range(6, NCH)] + ([] if last else [(i + 1, 0, k) for k in range(2)]),
                     None if first else ("D0", i - 1))
                slot([] if last else [(i + 1, 0, k) for k in range(2, 6)], ("b", i))
                if not first:
                    channel_sums(i - 1)
                slot([] if last else [(i + 1, 0, k) for k in range(6, NCH)] + [(i + 1, 1, k) for k in range(2)],
                     ("D1", i), None if first else lambda: window_means(i - 1))

            for k in range(NCH):
                diagonals(0, 0, k, fresh=(k < 2))
            for k in range(2):
                diagonals(0, 1, k)
            round_(0, first=True)
            with pool.Fori(1, ITERS - 1) as i:
                round_(i)
            round_(ITERS - 1, last=True)
            slot([], ("D0", ITERS - 1))
            channel_sums(ITERS - 1)
            window_means(ITERS - 1)

        @block.scalar
        def _(act):
            act.dma_start(cst[:, :], columns).then_inc(s_const, 16)
            act.dma_start(cw, cw_t.rearrange("(c p) m -> p c m", p=128)).then_inc(s_cw, 16)
            act.dma_start(tm[:, :], taps.to_broadcast([128, 2 * (N1 + N2) + 6])).then_inc(s_const, 16)
            act.sem_inc(s_uev, START)
            act.sem_inc(s_vev, START)
            act.sem_inc(s_tmp, START)
            act.sem_inc(s_l1e, START)
            def x_sums(k):
                n = k * BATCH + 1
                act.wait_ge(s_x[n], 16)
                if k:
                    act.wait_ge(s_gout, k)
                for c in range(NC2):
                    src = xs[:, (n * NC2 + c) * HW:(n * NC2 + c + 1) * HW]
                    for e, (func, scale, dst) in enumerate(((ACT.Copy, 1.0 / HW, mv[:, n, c, 0:1]),
                                                            (ACT.Square, HW ** -0.5, gin[:, 1, c, 1:2]))):
                        m = 4 * k + 2 * c + e
                        if m >= 2:
                            act.wait_ge(s_xs, m - 1)
                        act.activation(junkl[m % 2], src, func, scale=scale, accum_out=dst).then_inc(s_xs, 1)

            def store_f(k):
                for pr, src in ((k, pu), (ITERS + k, pv)):
                    p = 0 if src is pu else 1
                    act.wait_ge(s_fmm, 2 * k + p + 1)
                    act.wait_ge(s_fbias, 2 * (k + 1))
                    bias = fbias[:, 2 * (k % 2) + p:2 * (k % 2) + p + 1]
                    act.activation(shifted(fpad, pr * PAIR, INTERIOR), image(src[:, :]), ACT.Relu,
                                   bias=bias).then_inc(s_fev, 1)

            def hi_a(i, first=False):
                if not first:
                    act.wait_ge(s_pass, START + i * (2 * NCH) - NCH)
                act.activation(hl[0][LO, 0:PADDED], fpad[LO, bass.ds((i + ITERS) * PAIR, PADDED)],
                               ACT.Copy).then_inc(s_hi[0], 1)

            def hi_b(i, first=False):
                if not first:
                    act.wait_ge(s_pass, START + i * (2 * NCH))
                for parts in (HI, LO):
                    act.activation(hl[1][parts, 0:PADDED], fpad[HI, bass.ds((i + ITERS) * PAIR, PADDED)],
                                   ACT.Copy).then_inc(s_hi[1], 1)

            def store_u(i, m):
                act.wait_ge(s_pass, START + i * (2 * NCH) + (m * NCH + UCH))
                act.activation(uv[:, 0:HW], pu[:, :], ACT.Copy).then_inc(s_uev, 1)

            def store_v(i, m):
                act.wait_ge(s_pass, START + i * (2 * NCH) + (m * NCH + NCH))
                act.activation(uv[:, HW:2 * HW], pv[:, :], ACT.Copy).then_inc(s_vev, 1)

            def fused(what, i, beside=None):
                first = START + place(what, i)
                n = i * BATCH + SLOT_OF[what]
                for u in range(4):
                    act.wait_ge(s_fuse, first + (u + 1))
                    act.wait_ge(s_add, at_least(START, first + (u - 1)))
                    col = accg[:, bass.ds(n * 4 + u, 1)] if u % 2 == 0 else acc1[:, bass.ds(n * 2 + u // 2, 1)]
                    act.activation(tmp[u % 2][:, :], pf[:, (u % 2) * HALF:(u % 2 + 1) * HALF], ACT.Identity,
                                   bias=fb[:, u // 2:u // 2 + 1], accum_out=col).then_inc(s_tmp, 1)
                    if beside:
                        beside(u)

            def statistic(n, piece, q, before):
                if not isinstance(before, int) or before + q >= 2:
                    act.wait_ge(s_stat, before + (q - 1))
                if piece < NC2:
                    act.activation(junk[q % 2][:, 0:HW], xs[:, bass.ds((n * NC2 + piece) * HW, HW)], ACT.Square,
                                   bias=nwb[:, piece:piece + 1],
                                   accum_out=accg[:, bass.ds(n * 4 + (2 * piece + 1), 1)]).then_inc(s_stat, 1)
                else:
                    c, w = (piece - 2) // 4, (piece - 2) % 4
                    r, col = 4 + 8 * (w // 2), 4 + 8 * (w % 2)
                    img = image(xs[:, bass.ds((n * NC2 + c) * HW, HW)])
                    act.activation(junk[q % 2][:, 0:KEYS].rearrange("p (r c) -> p r c", c=WIN),
                                   img[:, r:r + WIN, col:col + WIN], ACT.Copy, scale=1.0 / KEYS,
                                   accum_out=acc_w[:, bass.ds(n * 8 + (4 * c + w), 1)]).then_inc(s_stat, 1)

            def stats(what, i, u):
                if u == 0:
                    act.wait_ge(s_add, START + place(what, i) + 4)
                q = sum(len(p) for p in PIECES[:u])
                for piece in PIECES[u]:
                    statistic(i * BATCH + SLOT_OF[what], piece, q, stats_before(what, i))
                    q += 1

            def first_tap2(i):
                act.wait_ge(s_gdi, i + 1)
                act.activation(image(yd[1][:, :]), shifted(fpad, i * PAIR, OFFSET[NA]), ACT.Copy,
                               scale=gdi[:, N1:N1 + 1]).then_inc(s_tap0, 1)

            def group_stats(i):
                act.wait_ge(s_l1g, i + 1)
                act.activation(l1[:, 0:16], pu[:, 0:16], ACT.Copy, scale=1.0 / HW).then_inc(s_l1e, 1)

            def inner_vectors(i):
                act.wait_ge(s_vec, i + 1)
                act.wait_ge(s_inner, START + i * BATCH)
                act.activation(l1[:, 104:136], pu[:, HALF:HALF + 32], ACT.Copy).then_inc(s_l1e, 1)

            def round_(i, first=False, last=False):
                def slot0(u):
                    if not first:
                        stats("D1", i - 1, u)
                    if u == 1 and not last:
                        hi_a(i + 1)

                def slot2(u):
                    if not first:
                        stats("D0", i - 1, u)
                    if u == 1 and not last:
                        hi_b(i + 1)

                def slot3(u):
                    stats("b", i, u)
                    if not first and u == 1:
                        group_stats(i - 1)

                store_v(i, 0)
                fused("a", i, slot0)
                store_u(i, 1)
                if first:
                    for u in range(4):
                        stats("a", i, u)
                else:
                    fused("D0", i - 1, lambda u: stats("a", i, u))
                store_v(i, 1)
                fused("b", i, slot2)
                if not last:
                    store_u(i + 1, 0)
                fused("D1", i, slot3)
                if not last:
                    first_tap2(i + 1)
                if not first:
                    inner_vectors(i - 1)

            act.wait_ge(s_zero, 1)
            x_sums(0)
            for k in range(1, ITERS):
                x_sums(k)
                store_f(k - 1)
                if k == 2:
                    hi_a(0, first=True)
                    hi_b(0, first=True)
            act.wait_ge(s_atm, 1)
            act.activation(at[:, :], pd[:, 0:NC2 * C], ACT.Copy).then_inc(s_at, 1)
            store_f(ITERS - 1)
            act.wait_ge(s_gw, 6)
            first_tap2(0)
            act.wait_ge(s_fb, 1)
            store_u(0, 0)
            act.wait_ge(s_hl[0], 1)
            act.wait_ge(s_hl[1], 1)
            round_(0, first=True)
            with act.Fori(1, ITERS - 1) as i:
                round_(i)
            round_(ITERS - 1, last=True)
            fused("D0", ITERS - 1, lambda u: stats("D1", ITERS - 1, u))
            for u in range(4):
                stats("D0", ITERS - 1, u)
            group_stats(ITERS - 1)
            inner_vectors(ITERS - 1)

        @block.vector
        def _(dve):
            steps = [0]

            def link(ins):
                steps[0] += 1
                ins.then_inc(s_dve, 1)
                dve.wait_ge(s_dve, steps[0])

            dve.sem_inc(s_yd, START)
            dve.sem_inc(s_inner, START)

            def lo_a(i):
                dve.wait_ge(s_hi[0], i + 1)
                dve.tensor_tensor(hl[0][HI, 0:PADDED], fpad[LO, bass.ds((i + ITERS) * PAIR, PADDED)],
                                  hl[0][LO, 0:PADDED].bitcast(F32), ALU.subtract).then_inc(s_hl[0], 1)

            def lo_b(i):
                dve.wait_ge(s_hi[1], i * 2 + 2)
                dve.tensor_tensor(hl[1][HI, 0:PADDED], fpad[HI, bass.ds((i + ITERS) * PAIR, PADDED)],
                                  hl[1][HI, 0:PADDED].bitcast(F32), ALU.subtract).then_inc(s_hl[1], 1)

            def group_sums(k):
                m = mv[:, k * BATCH:(k + 1) * BATCH, :, :]
                for js in (slice(0, 1), slice(2, 4)):
                    link(dve.tensor_tensor(gin[:, js, :, 1], m[:, js, :, 0], m[:, js, :, 0], ALU.mult))
                    link(dve.tensor_tensor(gin[:, js, :, 1], gin[:, js, :, 1], m[:, js, :, 1], ALU.add))
                dve.wait_ge(s_xs, 4 * (k + 1))
                dve.tensor_copy(gin[:, :, :, 0], m[:, :, :, 0]).then_inc(s_gin, 1)

            def variance(k):
                dve.wait_ge(s_gout, k + 1)
                link(dve.tensor_copy(yd[0][:, 16:32], pf[:, 0:16]))
                link(dve.tensor_tensor(vareps, gout[:, :, :, 0], gout[:, :, :, 0], ALU.mult))
                link(dve.tensor_tensor(vareps, gout[:, :, :, 1], vareps, ALU.subtract))
                dve.tensor_scalar(vareps, vareps, EPS, None, ALU.add).then_inc(s_var, 1)

            def scale(k):
                dve.wait_ge(s_rstd, k + 1)
                dve.wait_ge(s_cw, 16)
                dve.tensor_tensor(gmr.rearrange("p c j -> p j c"), gout[:, :, :, 0], rstd, ALU.mult).then_inc(s_gmr, 1)
                if k >= 2:
                    dve.wait_ge(s_fmm, 2 * (k - 1))
                dve.tensor_tensor(wsc[k % 2], cw[:, :, 0:CM].unsqueeze(2).to_broadcast([128, NC2, BATCH, CM]),
                                  rstd.rearrange("p j c -> p c j").unsqueeze(3).to_broadcast([128, NC2, BATCH, CM]),
                                  ALU.mult).then_inc(s_wsc, 1)
                g = gm[:, :, k * BATCH:(k + 1) * BATCH]
                m = mv[:, k * BATCH:(k + 1) * BATCH, :, 0].rearrange("p j c -> p c j")
                link(dve.tensor_tensor(g, m, rstd.rearrange("p j c -> p c j"), ALU.mult))
                dve.tensor_tensor(g, g, gmr, ALU.subtract).then_inc(s_gm, 1)

            def f_bias(k):
                dve.wait_ge(s_pbias, k + 1)
                if k >= 2:
                    dve.wait_ge(s_fev, 2 * (k - 1))
                f = fbias[:, 2 * (k % 2):2 * (k % 2) + 2]
                for parts, first in ((LO, 0), (HI, 1)):
                    dve.tensor_scalar(f[parts, :], pf[parts, HALF + first:HALF + 4:2], -1.0, cb[parts, :],
                                      ALU.mult, ALU.add).then_inc(s_fbias, 1)

            for k in range(ITERS):
                for slot, j in enumerate((0, 2, 3)):
                    n = k * BATCH + j
                    dve.wait_ge(s_x[n], 16)
                    for c in range(NC2):
                        for h in range(2):
                            base = (n * NC2 + c) * HW + h * HALF
                            ins = dve.bn_stats(bst[:, j, c, h, :], xs[:, base:base + HALF])
                    link(ins)
                    for c in range(NC2):
                        ins = dve.bn_aggr(mv[:, n, c, :], bst[:, j, c, :, :].rearrange("p h s -> p (h s)"))
                    link(ins)
                    if k >= 1:
                        (variance, scale, f_bias)[slot](k - 1)
                group_sums(k)
                if k == 0:
                    dve.wait_ge(s_const, 32)
                    link(dve.tensor_scalar(nwb[:, :], wb, -1.0, None, ALU.mult))
            lo_a(0)
            lo_b(0)
            k = ITERS - 1
            variance(k)
            scale(k)
            f_bias(k)

            dve.wait_ge(s_gmm, 1)
            link(dve.tensor_scalar(gall, pf[:, 64:64 + N], cb, 0.0, ALU.add, ALU.max))
            link(dve.reduce_sum(gbar[:, 0:1], gall, AX.X))
            for kk in range(2):
                a, b, c = (mixv[:, 3 * kk + e:3 * kk + e + 1] for e in range(3))
                t0, t1 = (0, N1) if kk == 0 else (N1, N1 + N2)
                base = N1 + N2
                link(dve.tensor_scalar(gbar[:, 1:2], gbar[:, 0:1], 1.0 / N, b, ALU.mult, ALU.mult))
                link(dve.tensor_scalar(s12[:, kk, :], gall, a, gbar[:, 1:2], ALU.mult, ALU.add))
                link(dve.tensor_tensor(sm, a, b, ALU.add))
                link(dve.tensor_scalar(dt[:, t0:t1], tapv[:, base + t0:base + t1], sm, c, ALU.mult, ALU.add))
                for parts, first in ((LO, 0), (HI, 1)):
                    dve.tensor_copy(sd[parts, kk, :], s12[parts, kk, first::4]).then_inc(s_s12, 1)
            dve.wait_ge(s_s12, 4)
            gd3 = gd[:, :].rearrange("p (i t) -> p i t", i=ITERS)
            for kk in range(2):
                t0, t1 = (0, N1) if kk == 0 else (N1, N1 + N2)
                link(dve.tensor_tensor(gd3[:, :, t0:t1], tapv[:, t0:t1].unsqueeze(1).to_broadcast([128, ITERS, t1 - t0]),
                                       sd[:, kk, :].unsqueeze(2).to_broadcast([128, ITERS, t1 - t0]), ALU.mult))
            link(dve.tensor_tensor(gd3, gd3, dt.unsqueeze(1).to_broadcast([128, ITERS, N1 + N2]), ALU.add))
            dve.tensor_scalar(gd[:, :], gd[:, :], 0.0, None, ALU.max).then_inc(s_gd, 1)
            link(dve.tensor_tensor(fb, fb, wb, ALU.add))
            dve.tensor_tensor(fb, pf[:, 96:96 + NC2], fb, ALU.add).then_inc(s_fb, 1)
            base_steps = steps[0]

            PER = NA + 2 * (N2 - 1) - 1

            def taps(i, second, first_pair=False, split_a=False):
                n = [NA if second else 0]

                def chained(ins, back):
                    n[0] += 1
                    ins.then_inc(s_dve, 1)
                    dve.wait_ge(s_dve, i * PER + (base_steps + n[0] - back))

                base = i * PAIR
                acc1 = image(pd[:, :])
                acc2 = image(yd[1][:, :])

                def tap1(t, parts=slice(0, 128), dst=acc1):
                    f, g = shifted(fpad, base, OFFSET[t], parts), gdi[parts, t:t + 1]
                    return dve.scalar_tensor_tensor(out=dst, in0=f, scalar=g, in1=acc1[parts],
                                                    op0=ALU.mult, op1=ALU.add)

                def tap2(j, parts=slice(0, 128), dst=acc2):
                    f, g = shifted(fpad, base, OFFSET[NA + j], parts), gdi[parts, N1 + j:N1 + j + 1]
                    return dve.scalar_tensor_tensor(out=dst, in0=f, scalar=g, in1=acc2[parts],
                                                    op0=ALU.mult, op1=ALU.add)

                if not second:
                    dve.wait_ge(s_yd, START + i * 4)
                    dve.tensor_copy(gdi[:, :], gd[:, bass.ds(i * (N1 + N2), N1 + N2)]).then_inc(s_gdi, 1)
                    dve.wait_ge(s_gdi, i + 1)
                    chained(dve.tensor_scalar(acc1, shifted(fpad, base, OFFSET[0]), gdi[:, 0:1], None, ALU.mult), 0)
                    for t in range(1, NA):
                        chained(tap1(t), 0)
                    return
                dve.wait_ge(s_tap0, i + 1)
                for j in range(N2 - 1):
                    if j:
                        chained(tap2(j), 1)
                    chained(tap1(NA + j), 1)
                    if j == 2 and split_a:
                        lo_a(i + 1)
                assert n[0] == PER
                dve.wait_ge(s_dve, i * PER + (base_steps + PER))
                if not first_pair:
                    dve.wait_ge(s_fuse, START + place("D0", i - 1) + 4)
                tap2(N2 - 1, LO, image(yd[0][HI, :])).then_inc(s_yd, 1)
                tap2(N2 - 1, HI, image(yd[1][HI, :])).then_inc(s_yd, 1)
                tap1(N1 - 1, LO, image(yd[0][LO, :])).then_inc(s_yd, 1)
                dve.wait_ge(s_yd, START + i * 4 + 1)
                tap1(N1 - 1, HI, image(yd[1][LO, :])).then_inc(s_yd, 1)

            def inner_blocks(i):
                dve.wait_ge(s_l1e, START + i * 2 + 2)
                for j in range(BATCH):
                    for c in range(NC2):
                        img = image(xs[:, bass.ds(((i * BATCH + j) * NC2 + c) * HW, HW)])
                        for b in range(2):
                            rows = img[:, IN0 + 8 * b:IN0 + 8 * b + 8, IN0:IN1].rearrange("p r (b c) -> p r b c", b=2)
                            add = vec[:, c, j, 2 * b:2 * b + 2].unsqueeze(1).unsqueeze(3)
                            ins = dve.tensor_tensor(rows, rows, add.to_broadcast([128, 8, 2, 8]), ALU.add)
                    ins.then_inc(s_inner, 1)

            dve.wait_ge(s_fev, 2 * ITERS)
            def round_(i, first=False):
                taps(i, True, first_pair=first, split_a=True)
                lo_b(i + 1)
                taps(i + 1, False)
                if not first:
                    inner_blocks(i - 1)

            taps(0, False)
            round_(0, first=True)
            with dve.Fori(1, ITERS - 1) as i:
                round_(i)
            taps(ITERS - 1, True)
            inner_blocks(ITERS - 2)
            inner_blocks(ITERS - 1)

        @block.tensor
        def _(pe):
            pe.sem_inc(s_pass, START)
            pe.sem_inc(s_fuse, START)
            pe.wait_ge(s_const, 32)
            pe.wait_ge(s_cw, 16)

            def groups(k):
                pe.wait_ge(s_gin, k + 1)
                pe.matmul(pf[:, 0:16], gmat, yd[0][:, 0:16], start=True, stop=True).then_inc(s_gout, 1)

            def f_batch(k):
                pe.wait_ge(s_gmr, k + 1)
                for c in range(NC2):
                    mm = pe.matmul(pf[:, HALF:HALF + 4], cw[:, c, :], gmr[:, c, :], start=(c == 0), stop=(c == NC2 - 1))
                mm.then_inc(s_pbias, 1)
                if k == ITERS - 1:
                    pe.wait_ge(s_gm, ITERS)
                    for c in range(NC2):
                        pe.matmul(pf[:, 64:64 + N], cw[:, c, :], gm[:, c, :], start=(c == 0), stop=(c == NC2 - 1))
                    for c in range(NC2):
                        mm = pe.matmul(pf[:, 96 + c:97 + c], fw[:, 128 * c:128 * (c + 1)], yb,
                                       start=True, stop=True)
                    mm.then_inc(s_gmm, 1)
                pe.wait_ge(s_wsc, k + 1)
                for p, dst in enumerate((pu, pv)):
                    if k >= 1:
                        pe.wait_ge(s_fev, 2 * (k - 1) + p + 1)
                    for h in range(2):
                        for c in range(NC2):
                            for m, parts in enumerate((LO, HI)):
                                j = 2 * p + m
                                at = ((k * BATCH + j) * NC2 + c) * HW + h * HALF
                                mm = pe.matmul(dst[parts, h * HALF:(h + 1) * HALF], wsc[k % 2][:, c, j, :],
                                               xs[:, at:at + HALF], start=(c == 0), stop=(c == NC2 - 1))
                    mm.then_inc(s_fmm, 1)

            for k in range(ITERS):
                groups(k)
                if k == ITERS - 1:
                    pe.wait_ge(s_attw, 32)
                    for c in range(NC2):
                        for e in range(NC2):
                            mm = pe.matmul(pd[:, C * c:C * (c + 1)], wv[:, C * e + 128 * c:C * e + 128 * (c + 1)],
                                           wot[:, C * e:C * (e + 1)], start=(e == 0), stop=(e == NC2 - 1))
                    mm.then_inc(s_atm, 1)
                f_batch(k)

            def chunk(i, m, k):
                q0, n = CHUNKS[k]
                j = m * NCH + k
                if k == 0:
                    pe.wait_ge(s_hl[m], i + 1)
                    pe.wait_ge(s_uev, START + i * 2 + m)
                if q0 == NA:
                    pe.wait_ge(s_vev, START + i * 2 + m)
                pe.wait_ge(s_diag, i * (2 * NCH) + (j + 1))
                dst = pu if q0 < NA else pv
                for q in range(q0, q0 + n):
                    lhs = wdiag[j % 2][:, (q - q0) * 128:(q - q0 + 1) * 128]
                    for h in range(2):
                        rhs = shifted(hl[m], 0, OFFSET[tap_of(q)], rows=slice(16 * h, 16 * h + 16))
                        mm = pe.matmul(dst[:, h * HALF:(h + 1) * HALF], lhs, rhs,
                                       start=(q in (0, NA)), stop=(q in (NA - 1, PASSES - 1)))
                mm.then_inc(s_pass, 1)

            def fuse(what, i, u):
                if u == 0 and what in "ab":
                    done = START + i * 2 + (1 if what == "a" else 2)
                    pe.wait_ge(s_uev, done)
                    pe.wait_ge(s_vev, done)
                if u == 0 and what == "D1":
                    pe.wait_ge(s_yd, START + i * 4 + 4)
                pe.wait_ge(s_tmp, at_least(START, START + place(what, i) + (u - 1)))
                c, h = u // 2, u % 2
                operands = {"D0": ((fw, yd[0]),), "D1": ((fw, yd[1]),)}.get(
                    what, ((fwu, uv[:, 0:HW]), (fw, uv[:, HW:2 * HW])))
                for e, (wt, y) in enumerate(operands):
                    mm = pe.matmul(pf[:, h * HALF:(h + 1) * HALF], wt[:, 128 * c:128 * (c + 1)],
                                   y[:, h * HALF:(h + 1) * HALF], start=(e == 0), stop=(e == len(operands) - 1))
                mm.then_inc(s_fuse, 1)

            def group_product(i, us):
                pe.wait_ge(s_sums, i + 1)
                pe.wait_ge(s_uev, START + us)
                pe.matmul(pu[:, 0:16], gmat, accg[:, bass.ds(i * 16, 16)],
                          start=True, stop=True).then_inc(s_l1g, 1)

            def attention(i):
                pe.wait_ge(s_gnw, i + 1)
                for o in range(NC2):
                    for c in range(NC2):
                        mm = pe.matmul(pu[:, HALF + 16 * o:HALF + 16 * (o + 1)],
                                       at[:, C * c + 128 * o:C * c + 128 * (o + 1)],
                                       l1[:, 72 + 16 * c:72 + 16 * (c + 1)], start=(c == 0), stop=(c == NC2 - 1))
                mm.then_inc(s_vec, 1)

            def slot(chunks, halves, beside=None):
                for n in range(max(len(chunks), 4)):
                    if n < len(chunks):
                        chunk(*chunks[n])
                    if halves and n < 4:
                        fuse(*halves, n)
                    if beside and n == 0:
                        beside()

            def round_(i, first=False, last=False):
                if not first:
                    pe.wait_ge(s_l1e, START + i * 2 - 2)
                slot([(i, 1, k) for k in range(UCH)], ("a", i))
                slot([(i, 1, k) for k in range(UCH, NCH)], None if first else ("D0", i - 1))
                slot([] if last else [(i + 1, 0, k) for k in range(UCH)], ("b", i))
                us = 2 * ITERS if last else i * 2 + 3
                slot([] if last else [(i + 1, 0, k) for k in range(UCH, NCH)], ("D1", i),
                     None if first else lambda: group_product(i - 1, us))
                if not first:
                    attention(i - 1)

            pe.wait_ge(s_fev, 2 * ITERS)
            pe.wait_ge(s_at, 1)
            pe.wait_ge(s_fb, 1)
            slot([(0, 0, k) for k in range(NCH)], None)
            round_(0, first=True)
            with pe.Fori(1, ITERS - 1) as i:
                round_(i)
            round_(ITERS - 1, last=True)
            for u in range(4):
                fuse("D0", ITERS - 1, u)
            group_product(ITERS - 1, 2 * ITERS)
            attention(ITERS - 1)


def kernel(**inputs):
    import concourse.bacc as bacc
    from concourse.bass_utils import run_bass_kernel_spmd as run

    a = {k: np.ascontiguousarray(v) for k, v in inputs.items()}
    k1, k2 = a["L0_conv_conv_kernel_w"].reshape(-1)[TAPS], a["L0_conv_conv_kernel2_w"].reshape(-1)
    b1, b2 = a["L0_conv_conv_kernel_b"][TAPS], a["L0_conv_conv_kernel2_b"]
    channel = np.arange(128)
    group_mean = (channel[:, None] // GROUP == channel[None, :] // GROUP).astype(np.float32) / GROUP
    ident = (channel[:, None] % CM == np.arange(CM)[None, :]).astype(np.float32)
    cw_t = a["L0_conv_conv_w"].reshape(CM, C).T
    fw_t = a["L0_conv_fuse_w"].reshape(C, 2 * CM).T
    conv_b = a["L0_conv_conv_b"].reshape(CM, 1)
    y_bias = np.concatenate([a["L0_conv_adap_bias"], a["L0_conv_atrous_bias"]]).reshape(2 * CM, 1)
    fuse_b = a["L0_conv_fuse_b"].reshape(NC2, 128).T
    wout_b = a["L1_conv_Wout_b"].reshape(NC2, 128).T
    arrays = {
        "x": a["x"],
        "cw_t": np.concatenate([cw_t, cw_t], 1),
        "taps": np.concatenate([k1, k2, b1, b2, a["L0_conv_conv_k_w"].reshape(-1), a["L0_conv_conv_k_b"],
                                a["L0_conv_conv_k2_w"].reshape(-1), a["L0_conv_conv_k2_b"]]).reshape(1, -1),
        "columns": np.concatenate([group_mean, ident, fw_t, np.concatenate([fw_t[:CM], fw_t[:CM]], 0),
                                   np.concatenate([conv_b, conv_b], 0), y_bias, fuse_b, wout_b], 1),
        "wkv": a["L1_conv_Wkv"],
        "wout_t": a["L1_conv_Wout_w"].T,
    }
    arrays = {k + "_dram": np.ascontiguousarray(v) for k, v in arrays.items()}
    nc = bacc.Bacc("TRN2", target_bir_lowering=False, num_devices=1)
    args = [nc.dram_tensor(k, v.shape, mybir.dt.from_np(v.dtype), kind="ExternalInput").ap()
            for k, v in arrays.items()]
    out = nc.dram_tensor("out_dram", (N, C, H, W), F32, kind="ExternalOutput").ap()
    build(nc, *args, out)
    return run(nc, [arrays], core_ids=[0]).results[0]["out_dram"]
```

```python
from contextlib import ExitStack

import numpy as np
import concourse.bass as bass
from concourse import mybir

F32 = mybir.dt.float32
F32R = mybir.dt.float32r
BF16 = mybir.dt.bfloat16
ALU = mybir.AluOpType
ACT = mybir.ActivationFunctionType
AX = mybir.AxisListType

N, C, H, W = 16, 256, 32, 32
HW = H * W
HALF = HW // 2
NC2 = C // 128
CM = 64
GROUP = 8
EPS = 1e-5
BATCH = 4
BATCHES = N // BATCH
PITCH = W + 2
PAIR = (H + 2) * PITCH
PADDED = (H + 4) * PITCH + 2
SPAN = H * PITCH
N1, N2 = 25, 9
SHARED = [5 * a + b for a in (0, 2, 4) for b in (0, 2, 4)]
ALONE = [t for t in range(N1) if t not in SHARED]
TAPS = ALONE + SHARED
NA = len(ALONE)
OFFSET = [(t // 5) * PITCH + t % 5 for t in TAPS]
PASSES = NA + 2 * N2
CHUNKS = [(q, min(4, PASSES - q)) for q in range(0, PASSES, 4)]
NCH = len(CHUNKS)
UCH = NA // 4
COLUMNS = 128 + CM + 2 * C + 2 + 2 * NC2
HALVES = 2 * NC2
STATS = 5 * NC2
PIECES = ((2, 3, 4), (0, 5), (6, 7, 8), (1, 9))
ALL, PAIR_D, PAIR_P = slice(0, BATCH), slice(0, 2), slice(2, BATCH)
START = 1
CHMAX = max(n for _, n in CHUNKS)
WIN = 16
KEYS = WIN * WIN
IN0, IN1 = 8, 24


def tap_of(q):
    return q if q < NA + N2 else q - N2


def build(nc, x, cw_t, taps, columns, wkv, wout_t, out):
    with ExitStack() as ctx:
        def sb(name, shape, dt=F32):
            return ctx.enter_context(nc.sbuf_tensor(name, shape, dt))

        def pb(name):
            return ctx.enter_context(nc.psum_tensor(name, [128, HW], F32))

        def sem(name):
            return ctx.enter_context(nc.semaphore(name))

        xs = sb("xs", [128, N * NC2 * HW])
        fpad = sb("fpad", [128, 7 * PAIR + 4 * PITCH + 4 + SPAN])
        hl = [sb(f"hl{b}", [128, PADDED + 2], F32R) for b in range(2)]
        wdiag = [sb(f"wdiag{b}", [128, CHMAX * 128], F32R) for b in range(2)]
        uv = sb("uv", [128, 2 * HW])
        yd = [sb(f"yd{b}", [128, HW]) for b in range(2)]
        tmp = [sb(f"tmp{b}", [128, HALF]) for b in range(2)]
        cst = sb("cst", [128, COLUMNS])
        gmat, eye = cst[:, 0:128], cst[:, 128:192]
        fw, fwu = cst[:, 192:448], cst[:, 448:704]
        cb, yb = cst[:, 704:705], cst[:, 705:706]
        fb = cst[:, 706:708]
        wb = cst[:, 708:710]
        tm = sb("tm", [128, 2 * (N1 + N2) + 6])
        tapv = tm[:, 0:2 * (N1 + N2)]
        mixv = tm[:, 2 * (N1 + N2):]
        nwb = sb("nwb", [128, NC2])
        nwbk = sb("nwbk", [128, NC2])
        mv = sb("mv", [128, N, NC2, 2])
        gm = sb("gm", [128, NC2, N])
        gw = sb("gw", [128, 2 * BATCH * PASSES * 2])
        gd = sb("gd", [128, BATCHES * (N1 + N2)])
        gdi = sb("gdi", [128, N1 + N2])
        accg = sb("accg", [128, N * NC2 * 2])
        acc1 = sb("acc1", [128, N * NC2])
        acc_w = sb("acc_w", [128, N * NC2 * 4])
        mvs = sb("mvs", [128, N * NC2])
        at = sb("at", [128, NC2 * C])
        minus_half = sb("minus_half", [128, NC2 * BATCH])
        eps = sb("eps", [128, 2])
        free_p = 4 * PAIR + 2 * PITCH + 2
        junk = [fpad[:, free_p + 512 * b:free_p + 512 * (b + 1)].bitcast(BF16) for b in range(2)]
        l1 = fpad[:, 2 * PITCH + 2:2 * PITCH + 162]
        gmean = l1[:, 0:8]
        e2 = l1[:, 8:16]
        l1v, l1r = l1[:, 16:24], l1[:, 24:32]
        cen = l1[:, 40:72].rearrange("p (j c w) -> p j c w", j=BATCH, c=NC2)
        gnw = l1[:, 72:104].rearrange("p (c j w) -> p c j w", c=NC2, j=BATCH)
        vec = l1[:, 104:136].rearrange("p (c j w) -> p c j w", c=NC2, j=BATCH)
        cw = uv[:, 0:256].rearrange("p (c m) -> p c m", c=NC2)
        wsc = [uv[:, 512 + 512 * b:1024 + 512 * b].rearrange("p (c j m) -> p c j m", c=NC2, j=BATCH)
               for b in range(2)]
        bst = uv[:, 1536:1536 + 24 * BATCH].rearrange("p (j c h s) -> p j c h s", j=BATCH, c=NC2, h=2)
        gin = [yd[0][:, o:o + 16].rearrange("p (j c s) -> p j c s", j=BATCH, c=NC2) for o in (0, 240)]
        gout = yd[0][:, 16:32].rearrange("p (j c s) -> p j c s", j=BATCH, c=NC2)
        vareps = yd[0][:, 32:40].rearrange("p (j c) -> p j c", j=BATCH)
        rstd = yd[0][:, 40:48].rearrange("p (j c) -> p j c", j=BATCH)
        gmr = yd[0][:, 48:56].rearrange("p (c j) -> p c j", c=NC2)
        fbias = yd[0][:, 96:104]
        gall = yd[0][:, 128:144]
        gsum = yd[0][:, 144:145]
        kdom = yd[0][:, 146:148]
        kab = yd[0][:, 148:150]
        s12 = yd[0][:, 160:192].rearrange("p (k n) -> p k n", k=2)
        sd = yd[0][:, 192:200].rearrange("p (k i) -> p k i", k=2)
        dt = yd[0][:, 200:234]
        gk, gkr, gkh = (t[:, o:o + 8 * (N1 + N2)] for t, o in ((tmp[0], 0), (tmp[1], 0), (yd[0], 512)))
        gk3, gkr3, gkh3 = (t.rearrange("p (n t) -> p n t", n=8) for t in (gk, gkr, gkh))
        wv = yd[1][:, 0:512]
        wot = yd[1][:, 512:1024]
        junkl = [tmp[b][:, :].bitcast(BF16) for b in range(2)]

        pu, pv, pf, pd = pb("pu"), pb("pv"), pb("pf"), pb("pd")

        s_const = sem("const_loaded")
        s_cw = sem("conv_w_loaded")
        s_x = [sem(f"x_loaded{n}") for n in range(N)]
        s_dve = sem("dve_step")
        s_pool = sem("pool_step")
        s_zero = sem("pads_zeroed")
        s_gin = sem("channel_stats_ready")
        s_gout = sem("group_stats_done")
        s_var = sem("variance_ready")
        s_rstd = sem("rstd_ready")
        s_gmr = sem("shift_ready")
        s_pbias = sem("shift_product_done")
        s_wsc = sem("scaled_weights_ready")
        s_fbias = sem("f_bias_ready")
        s_fmm = sem("f_products_done")
        s_fev = sem("f_stored")
        s_gmm = sem("g_product_done")
        s_s12 = sem("kernel_scales_ready")
        s_gk = sem("p_kernels_ready")
        s_gkr = sem("p_kernels_relued")
        s_gw = sem("kernel_values_ready")
        s_gm = sem("pixel_means_ready")
        s_gd = sem("d_values_ready")
        s_fb = sem("fusion_bias_ready")
        s_hi = [sem("hi_a_ready"), sem("hi_b_ready")]
        s_hl = [sem("hi_lo_a_ready"), sem("hi_lo_b_ready")]
        s_diag = sem("diagonals_ready")
        s_pass = sem("chunk_passed")
        s_uev, s_vev = sem("u_stored"), sem("v_stored")
        s_yd = sem("d_sums_ready")
        s_fuse = sem("fuse_half_done")
        s_tmp = sem("fused_half_in_tmp")
        s_add = sem("x1_half_ready")
        s_stat = sem("x1_statistic_done")
        s_xs = sem("x_sums_ready")
        s_tap0 = sem("first_taps_done")
        s_gdi = sem("pair_values_ready")
        s_attw = sem("attention_weights_loaded")
        s_atm = sem("attention_product_done")
        s_at = sem("attention_matrix_ready")
        s_addl = sem("last_pair_half_added")
        s_sums = sem("last_pair_measured")
        s_innerp = sem("inner_blocks_added_by_gpsimd")
        s_l1g = sem("x1_group_sums_done")
        s_l1e = sem("chain_part_stored")
        s_l1 = sem("chain_step")
        s_gnw = sem("window_means_ready")
        s_vec = sem("inner_vectors_done")
        s_inner = sem("inner_blocks_added")
        s_store = sem("stored")

        def xh(n, c, h):
            return xs[:, bass.ds((n * NC2 + c) * HW + h * HALF, HALF)]

        def shifted(tile, base, off, parts=slice(0, 128), rows=slice(0, H)):
            full = tile[parts, bass.ds(base + off + rows.start * PITCH, (rows.stop - rows.start) * PITCH)]
            return full.rearrange("p (r c) -> p r c", c=PITCH)[:, :, 0:W]

        def place(what, i):
            known = isinstance(i, int)
            if what == "a":
                return 0 if known and i == 0 else i * (BATCH * HALVES) - HALVES
            if what == "D0":
                return (N - 1) * HALVES if known and i == BATCHES - 1 else i * (BATCH * HALVES) + BATCH * HALVES
            return i * (BATCH * HALVES) + (1 if what == "b" else 2) * HALVES

        def stats_before(what, i):
            known = isinstance(i, int)
            if what == "a":
                return 0 if known and i == 0 else i * (BATCH * STATS) - STATS
            if what == "D0":
                return (N - 1) * STATS if known and i == BATCHES - 1 else i * (BATCH * STATS) + BATCH * STATS
            return i * (BATCH * STATS) + (1 if what == "b" else 2) * STATS

        def at_least(n, expr):
            return max(n, expr) if isinstance(expr, int) else expr

        SLOT_OF = {"D0": 0, "D1": 1, "a": 2, "b": 3}

        def image(ap):
            return ap.rearrange("p (r c) -> p r c", c=W)

        last_p, last_d = BATCHES - 1, BATCHES

        stored = START + 2 * (BATCHES - 2)

        def columns_of(js):
            return slice(NC2 * js.start, NC2 * js.stop)

        def inner_image(engine, i, j):
            for c in range(NC2):
                img = image(xs[:, bass.ds(((i * BATCH + j) * NC2 + c) * HW, HW)])
                for b in range(2):
                    rows = img[:, IN0 + 8 * b:IN0 + 8 * b + 8, IN0:IN1].rearrange("p r (b c) -> p r b c", b=2)
                    part = vec[:, c, j, 2 * b:2 * b + 2].unsqueeze(1).unsqueeze(3)
                    ins = engine.tensor_tensor(rows, rows, part.to_broadcast([128, 8, 2, 8]), ALU.add)
            return ins

        gw4 = gw[:, :].rearrange("p (n q s) -> p n q s", n=8, s=2)
        INTERIOR = 2 * PITCH + 2
        LO, HI = slice(0, 64), slice(64, 128)

        x_v = x.rearrange("n (c p) h w -> p (n c) (h w)", p=128)
        out_v = out.rearrange("n (c p) h w -> p (n c) (h w)", p=128)

        block = ctx.enter_context(nc.Block())

        @block.sync
        def _(sp):
            for n in range(N):
                sp.dma_start(xs[:, n * NC2 * HW:(n + 1) * NC2 * HW].rearrange("p (c f) -> p c f", c=NC2),
                             x_v[:, n * NC2:(n + 1) * NC2, :]).then_inc(s_x[n], 16)
            sp.dma_start(wv.rearrange("p (k c) -> p k c", k=2),
                         wkv[C:2 * C, :].rearrange("(k p) c -> p k c", p=128)).then_inc(s_attw, 16)
            sp.dma_start(wot.rearrange("p (k o) -> p k o", k=2),
                         wout_t.rearrange("(k p) o -> p k o", p=128)).then_inc(s_attw, 16)

            def store_rows(n, r0, r1):
                src = xs[:, bass.ds(n * NC2 * HW, NC2 * HW)].rearrange("p (c f) -> p c f", c=NC2)
                sp.dma_start(out_v[:, bass.ds(n * NC2, NC2), r0 * W:r1 * W],
                             src[:, :, r0 * W:r1 * W]).then_inc(s_store, 16)

            def outer_rows(what, i):
                sp.wait_ge(s_add, START + place(what, i) + HALVES)
                store_rows(i * BATCH + SLOT_OF[what], 0, IN0)
                store_rows(i * BATCH + SLOT_OF[what], IN1, H)

            def inner_rows(i):
                for j in range(BATCH):
                    sp.wait_ge(s_inner, START + i * BATCH + (j + 1))
                    store_rows(i * BATCH + j, IN0, IN1)

            def stores(i, first=False, last=False):
                outer_rows("a", i)
                if not first:
                    outer_rows("D0", i - 1)
                outer_rows("b", i)
                if not last:
                    outer_rows("D1", i)
                else:
                    for j in (1, 0):
                        sp.wait_ge(s_addl, 8 - 4 * j)
                        store_rows(i * BATCH + j, 0, IN0)
                        store_rows(i * BATCH + j, IN1, H)
                if not first and not last:
                    inner_rows(i - 1)

            stores(0, first=True)
            with sp.Fori(1, BATCHES - 1) as i:
                stores(i)
            stores(BATCHES - 1, last=True)
            base = START + N - 2 * BATCH
            for n, done, count in ((N - 8, s_innerp, 1), (N - 7, s_innerp, 2), (N - 6, s_inner, base + 1),
                                   (N - 5, s_inner, base + 2), (N - 2, s_inner, base + 3), (N - 1, s_inner, base + 4),
                                   (N - 4, s_inner, base + 5), (N - 3, s_innerp, 3)):
                sp.wait_ge(done, count)
                store_rows(n, IN0, IN1)
            sp.wait_ge(s_store, 16 * 3 * N)

        @block.gpsimd
        def _(pool):
            steps = [0]

            def link(ins):
                steps[0] += 1
                ins.then_inc(s_pool, 1)
                pool.wait_ge(s_pool, steps[0])

            pool.sem_inc(s_add, START)
            link(pool.memset(minus_half[:, :], -0.5))
            link(pool.memset(eps[:, :], EPS))
            pool.memset(fpad[:, :], 0.0).then_inc(s_zero, 1)
            for k in range(BATCHES):
                pool.wait_ge(s_var, k + 1)
                pool.tensor_tensor(yd[0][:, 40:48], yd[0][:, 32:40], minus_half[:, :], ALU.pow).then_inc(s_rstd, 1)
            m3 = mvs[:, :].rearrange("p (n c) -> p n c", c=NC2)
            pool.wait_ge(s_gm, BATCHES)
            link(pool.tensor_tensor(m3, mv[:, :, :, 0], wb.unsqueeze(1).to_broadcast([128, N, NC2]), ALU.subtract))
            link(pool.tensor_scalar(mvs[:, :], mvs[:, :], float(HW), None, ALU.mult))
            pool.wait_ge(s_s12, 2)
            for k in range(2):
                t0, t1 = (0, N1) if k == 0 else (N1, N1 + N2)
                for m in range(2):
                    ins = pool.tensor_tensor(
                        gk3[:, m::2, t0:t1], tapv[:, t0:t1].unsqueeze(1).to_broadcast([128, BATCHES, t1 - t0]),
                        s12[:, k, 2 + m::4].unsqueeze(2).to_broadcast([128, BATCHES, t1 - t0]), ALU.mult)
            link(ins)
            pool.tensor_tensor(gk3, gk3, dt.unsqueeze(1).to_broadcast([128, 8, N1 + N2]), ALU.add).then_inc(s_gk, 1)
            pool.wait_ge(s_gkr, 2)
            for q0, n, s, t0 in ((0, NA, 1, 0), (NA + N2, N2, 0, NA), (NA + N2, N2, 1, N1)):
                pool.tensor_tensor(gw4[:, :, q0:q0 + n, s], gkr3[:, :, t0:t0 + n], gkh3[:, :, t0:t0 + n],
                                   ALU.subtract).then_inc(s_gw, 1)
            pool.wait_ge(s_gw, 6)

            def diagonals(i, m, k, fresh=False):
                j = m * NCH + k
                q0, n = CHUNKS[k]
                if not fresh:
                    pool.wait_ge(s_pass, START + i * (2 * NCH) + (j - 1))
                vals = gw[:, bass.ds((i * 2 + m) * (2 * PASSES) + 2 * q0, 2 * n)]
                pool.tensor_tensor(wdiag[j % 2][:, 0:n * 128].rearrange("p (q m) -> p q m", m=CM),
                                   eye.unsqueeze(1).to_broadcast([128, 2 * n, CM]),
                                   vals.unsqueeze(2).to_broadcast([128, 2 * n, CM]), ALU.mult).then_inc(s_diag, 1)

            def add(what, i, u):
                pool.wait_ge(s_tmp, START + place(what, i) + (u + 1))
                dst = xh(i * BATCH + SLOT_OF[what], u // 2, u % 2)
                pool.tensor_tensor(dst, tmp[u % 2][:, :], dst, ALU.add).then_inc(s_add, 1)

            def inverse_deviation(n, js=ALL):
                cols = columns_of(js)
                pool.tensor_tensor(l1v[:, cols], e2[:, cols], l1v[:, cols], ALU.subtract).then_inc(s_l1, 1)
                pool.wait_ge(s_l1, n * 3 + 1)
                pool.tensor_tensor(l1r[:, cols], l1v[:, cols], minus_half[:, cols], ALU.pow).then_inc(s_l1, 1)

            def window_means(n, js=ALL, i=None):
                cols, i = columns_of(js), n if i is None else i
                size = cols.stop - cols.start
                pool.tensor_tensor(cen.rearrange("p j c w -> p (j c) w")[:, cols, :],
                                   acc_w[:, bass.ds(i * 32 + 4 * cols.start, 4 * size)].rearrange(
                                       "p (n w) -> p n w", w=4),
                                   gmean[:, cols].unsqueeze(2).to_broadcast([128, size, 4]), ALU.subtract).then_inc(s_l1, 1)
                pool.wait_ge(s_l1, n * 3 + 3)
                pool.tensor_tensor(gnw.rearrange("p c j w -> p j c w")[:, js], cen[:, js],
                                   l1r[:, cols].rearrange("p (j c) -> p j c", c=NC2).unsqueeze(3).to_broadcast(
                                       [128, size // NC2, NC2, 4]), ALU.mult).then_inc(s_gnw, 1)

            def slot(chunks, halves, chain=None):
                def diagonal(n):
                    if n < len(chunks):
                        diagonals(*chunks[n])

                def half(u):
                    if halves:
                        add(*halves, u)

                diagonal(0)
                half(0)
                diagonal(1)
                if chain is not None:
                    pool.wait_ge(s_l1e, START + chain * 2 + 1)
                    inverse_deviation(chain)
                    window_means(chain)
                half(1)
                diagonal(2)
                diagonal(3)
                half(2)
                half(3)
                diagonal(4)

            def round_(i, first=False, last=False):
                slot([(i, 1, k) for k in range(2, 6)], ("a", i))
                slot([(i, 1, k) for k in range(6, NCH)] + ([] if last else [(i + 1, 0, k) for k in range(2)]),
                     None if first else ("D0", i - 1))
                slot([] if last else [(i + 1, 0, k) for k in range(2, 6)], ("b", i))
                if last:
                    return
                slot([(i + 1, 0, k) for k in range(6, NCH)] + [(i + 1, 1, k) for k in range(2)],
                     ("D1", i), None if first else i - 1)

            for k in range(NCH):
                diagonals(0, 0, k, fresh=(k < 2))
            for k in range(2):
                diagonals(0, 1, k)
            round_(0, first=True)
            with pool.Fori(1, BATCHES - 1) as i:
                round_(i)
            round_(BATCHES - 1, last=True)
            pool.wait_ge(s_l1e, stored + 1)
            inverse_deviation(BATCHES - 2)
            window_means(BATCHES - 2)
            pool.wait_ge(s_l1e, stored + 2)
            for j in (0, 1):
                inner_image(pool, BATCHES - 2, j).then_inc(s_innerp, 1)
            pool.wait_ge(s_l1e, stored + 3)
            inverse_deviation(last_p, PAIR_P)
            window_means(last_p, PAIR_P)
            pool.wait_ge(s_l1e, stored + 4)
            inverse_deviation(last_d, PAIR_D)
            pool.wait_ge(s_stat, STATS * (N - 2) + 12)
            pool.wait_ge(s_sums, 3)
            window_means(last_d, PAIR_D, BATCHES - 1)
            pool.wait_ge(s_l1e, stored + 6)
            inner_image(pool, BATCHES - 1, 1).then_inc(s_innerp, 1)

        @block.scalar
        def _(act):
            act.dma_start(cst[:, :], columns).then_inc(s_const, 16)
            act.dma_start(cw, cw_t.rearrange("(c p) m -> p c m", p=128)).then_inc(s_cw, 16)
            act.dma_start(tm[:, :], taps.to_broadcast([128, 2 * (N1 + N2) + 6])).then_inc(s_const, 16)
            act.sem_inc(s_uev, START)
            act.sem_inc(s_vev, START)
            act.sem_inc(s_tmp, START)
            act.sem_inc(s_l1e, START)

            def x_sums(k, j):
                n = k * BATCH + j
                act.wait_ge(s_x[n], 16)
                if k >= 2 and j == 0:
                    act.wait_ge(s_gout, k - 1)
                for c in range(NC2):
                    src = xs[:, (n * NC2 + c) * HW:(n * NC2 + c + 1) * HW]
                    for e, (func, scale, dst) in enumerate(((ACT.Copy, 1.0 / HW, mv[:, n, c, 0:1]),
                                                            (ACT.Square, HW ** -0.5, gin[k % 2][:, j, c, 1:2]))):
                        m = 8 * k + 2 * j + 2 * c + e
                        if m >= 2:
                            act.wait_ge(s_xs, m - 1)
                        act.activation(junkl[m % 2], src, func, scale=scale, accum_out=dst).then_inc(s_xs, 1)

            def store_f(k, p):
                act.wait_ge(s_fmm, 2 * k + p + 1)
                act.wait_ge(s_fbias, 2 * (k + 1))
                bias = fbias[:, 2 * (k % 2) + p:2 * (k % 2) + p + 1]
                act.activation(shifted(fpad, (p * BATCHES + k) * PAIR, INTERIOR), image((pu, pv)[p][:, :]), ACT.Relu,
                               bias=bias).then_inc(s_fev, 1)

            def hi_a(i, first=False):
                if not first:
                    act.wait_ge(s_pass, START + i * (2 * NCH) - NCH)
                act.activation(hl[0][LO, 0:PADDED], fpad[LO, bass.ds((i + BATCHES) * PAIR, PADDED)],
                               ACT.Copy).then_inc(s_hi[0], 1)

            def hi_b(i, first=False):
                if not first:
                    act.wait_ge(s_pass, START + i * (2 * NCH))
                for parts in (HI, LO):
                    act.activation(hl[1][parts, 0:PADDED], fpad[HI, bass.ds((i + BATCHES) * PAIR, PADDED)],
                                   ACT.Copy).then_inc(s_hi[1], 1)

            def store_u(i, m):
                act.wait_ge(s_pass, START + i * (2 * NCH) + (m * NCH + UCH))
                act.activation(uv[:, 0:HW], pu[:, :], ACT.Copy).then_inc(s_uev, 1)

            def store_v(i, m):
                act.wait_ge(s_pass, START + i * (2 * NCH) + (m * NCH + NCH))
                act.activation(uv[:, HW:2 * HW], pv[:, :], ACT.Copy).then_inc(s_vev, 1)

            def fused(what, i, beside=None):
                first = START + place(what, i)
                j = SLOT_OF[what]
                for u in range(4):
                    act.wait_ge(s_fuse, first + (u + 1))
                    act.wait_ge(s_add, at_least(START, first + (u - 1)))
                    n = j * NC2 + u // 2
                    col = accg[:, bass.ds(i * 16 + n, 1)] if u % 2 == 0 else acc1[:, bass.ds(i * 8 + n, 1)]
                    act.activation(tmp[u % 2][:, :], pf[:, (u % 2) * HALF:(u % 2 + 1) * HALF], ACT.Identity,
                                   bias=fb[:, u // 2:u // 2 + 1], accum_out=col).then_inc(s_tmp, 1)
                    if beside:
                        beside(u)

            def statistic(i, j, piece, q, before):
                if not isinstance(before, int) or before + q >= 2:
                    act.wait_ge(s_stat, before + (q - 1))
                if piece < NC2:
                    src = xs[:, bass.ds(((i * BATCH + j) * NC2 + piece) * HW, HW)]
                    act.activation(junk[q % 2][:, 0:HW], src, ACT.Square, bias=nwb[:, piece:piece + 1],
                                   accum_out=accg[:, bass.ds(i * 16 + (8 + j * NC2 + piece), 1)]).then_inc(s_stat, 1)
                else:
                    c, w = (piece - 2) // 4, (piece - 2) % 4
                    r, col = 4 + 8 * (w // 2), 4 + 8 * (w % 2)
                    img = image(xs[:, bass.ds(((i * BATCH + j) * NC2 + c) * HW, HW)])
                    act.activation(junk[q % 2][:, 0:KEYS].rearrange("p (r c) -> p r c", c=WIN),
                                   img[:, r:r + WIN, col:col + WIN], ACT.Identity, scale=1.0 / KEYS,
                                   bias=nwbk[:, c:c + 1],
                                   accum_out=acc_w[:, bass.ds(i * 32 + ((j * NC2 + c) * 4 + w), 1)]).then_inc(s_stat, 1)

            def stats(what, i, u, before=None):
                if u == 0:
                    act.wait_ge(s_add, START + place(what, i) + HALVES)
                q = sum(len(p) for p in PIECES[:u])
                for piece in PIECES[u]:
                    statistic(i, SLOT_OF[what], piece, q, stats_before(what, i) if before is None else before)
                    q += 1

            def first_tap2(i):
                act.wait_ge(s_gdi, i + 1)
                act.activation(image(yd[1][:, :]), shifted(fpad, i * PAIR, OFFSET[NA]), ACT.Copy,
                               scale=gdi[:, N1:N1 + 1]).then_inc(s_tap0, 1)

            def group_stats(n, js=ALL):
                act.wait_ge(s_l1g, n + 1)
                cols = columns_of(js)
                mean, squares = pu[:, cols], pu[:, 8 + cols.start:8 + cols.stop]
                act.activation(gmean[:, cols], mean, ACT.Copy, scale=1.0 / HW)
                act.activation(l1v[:, cols], mean, ACT.Square, scale=1.0 / HW)
                act.activation(e2[:, cols], squares, ACT.Identity, scale=1.0 / HW, bias=eps[:, 0:1]).then_inc(s_l1e, 1)

            def inner_vectors(n, js=ALL, src=pf[:, 0:32]):
                act.wait_ge(s_vec, n + 1)
                act.activation(vec[:, :, js, :], src.rearrange("p (c j w) -> p c j w", c=NC2, j=BATCH)[:, :, js, :],
                               ACT.Copy).then_inc(s_l1e, 1)

            def round_(i, first=False, last=False):
                def slot0(u):
                    if u == 0 and not first:
                        first_tap2(i)
                    if u == 1 and not last:
                        hi_a(i + 1)
                    if not first:
                        stats("D1", i - 1, u)

                def slot1(u):
                    if u < 3:
                        stats("a", i, u)

                def slot2(u):
                    if u == 0 and not last:
                        hi_b(i + 1)
                    if not first:
                        stats("D0", i - 1, u, before=stats_before("D0", i - 1) - 2 if last else None)

                def slot3(u):
                    if u < 3:
                        stats("b", i, u)
                    if u == 0 and not first:
                        group_stats(i - 1)

                fused("a", i, slot0)
                store_u(i, 1)
                if first:
                    for u in range(3):
                        slot1(u)
                else:
                    fused("D0", i - 1, slot1)
                store_v(i, 1)
                if not last:
                    stats("a", i, 3)
                fused("b", i, slot2)
                if last:
                    return
                store_u(i + 1, 0)
                fused("D1", i, slot3)
                store_v(i + 1, 0)
                if not first:
                    act.wait_ge(s_inner, START + i * BATCH - BATCH)
                    inner_vectors(i - 1)
                stats("b", i, 3)

            act.wait_ge(s_zero, 1)
            for step, k, p in ((x_sums, 0, 0), (x_sums, 0, 2), (x_sums, 1, 0), (x_sums, 1, 2), (x_sums, 2, 0),
                               (store_f, 0, 0), (store_f, 0, 1), (x_sums, 2, 2), (x_sums, 3, 0),
                               (store_f, 1, 0), (store_f, 1, 1), (x_sums, 3, 2)):
                step(k, p)
            hi_a(0, first=True)
            store_f(2, 0)
            store_f(2, 1)
            act.wait_ge(s_atm, 1)
            act.activation(at[:, :], pd[:, 0:NC2 * C], ACT.Copy).then_inc(s_at, 1)
            hi_b(0, first=True)
            act.wait_ge(s_gk, 1)
            act.activation(gkh.bitcast(F32R), gk, ACT.Relu).then_inc(s_gkr, 1)
            act.activation(gkr, gk, ACT.Relu).then_inc(s_gkr, 1)
            act.wait_ge(s_gkr, 1)
            for q0, n, s, t0 in ((0, NA, 0, 0), (NA, N2, 0, NA), (NA, N2, 1, N1)):
                act.activation(gw4[:, :, q0:q0 + n, s], gkh3[:, :, t0:t0 + n], ACT.Copy).then_inc(s_gw, 1)
            store_f(3, 0)
            store_f(3, 1)
            first_tap2(0)
            act.wait_ge(s_gw, 6)
            act.wait_ge(s_fb, 1)
            store_u(0, 0)
            act.wait_ge(s_hl[0], 1)
            act.wait_ge(s_hl[1], 1)
            store_v(0, 0)
            round_(0, first=True)
            with act.Fori(1, BATCHES - 1) as i:
                round_(i)
            round_(BATCHES - 1, last=True)
            group_stats(BATCHES - 2)
            stats("a", BATCHES - 1, 3, before=stats_before("b", BATCHES - 1) - STATS)
            for u in range(4):
                if u == 3:
                    act.wait_ge(s_inner, START + (BATCHES - 2) * BATCH)
                    inner_vectors(BATCHES - 2, src=pu[:, HALF:HALF + 32])
                stats("b", BATCHES - 1, u)
            act.wait_ge(s_addl, 4)
            for q in range(8):
                if q == 2:
                    group_stats(last_p, PAIR_P)
                if q == 6:
                    group_stats(last_d, PAIR_D)
                statistic(BATCHES - 1, 1, 2 + q, q, STATS * (N - 2))
            act.wait_ge(s_inner, START + N - 2 * BATCH + 2)
            inner_vectors(last_p, PAIR_P, pu[:, HALF:HALF + 32])
            act.wait_ge(s_addl, 8)
            for q in range(4):
                statistic(BATCHES - 1, 0, 6 + q, 8 + q, STATS * (N - 2))
            act.wait_ge(s_innerp, 2)
            inner_vectors(last_d, PAIR_D, pu[:, HALF:HALF + 32])

        @block.vector
        def _(dve):
            steps = [0]

            def link(ins):
                steps[0] += 1
                ins.then_inc(s_dve, 1)
                dve.wait_ge(s_dve, steps[0])

            dve.sem_inc(s_yd, START)
            dve.sem_inc(s_inner, START)

            def lo_a(i):
                dve.wait_ge(s_hi[0], i + 1)
                dve.tensor_tensor(hl[0][HI, 0:PADDED], fpad[LO, bass.ds((i + BATCHES) * PAIR, PADDED)],
                                  hl[0][LO, 0:PADDED].bitcast(F32), ALU.subtract).then_inc(s_hl[0], 1)

            def lo_b(i):
                dve.wait_ge(s_hi[1], i * 2 + 2)
                dve.tensor_tensor(hl[1][HI, 0:PADDED], fpad[HI, bass.ds((i + BATCHES) * PAIR, PADDED)],
                                  hl[1][HI, 0:PADDED].bitcast(F32), ALU.subtract).then_inc(s_hl[1], 1)

            def x_stats(k, j):
                n = k * BATCH + j
                dve.wait_ge(s_x[n], 16)
                for c in range(NC2):
                    for h in range(2):
                        base = (n * NC2 + c) * HW + h * HALF
                        ins = dve.bn_stats(bst[:, j, c, h, :], xs[:, base:base + HALF])
                link(ins)
                for c in range(NC2):
                    ins = dve.bn_aggr(mv[:, n, c, :], bst[:, j, c, :, :].rearrange("p h s -> p (h s)"))
                link(ins)

            def group_sums(k):
                m = mv[:, k * BATCH:(k + 1) * BATCH, :, :]
                mine, g = slice(1, BATCH, 2), gin[k % 2]
                link(dve.tensor_tensor(g[:, mine, :, 1], m[:, mine, :, 0], m[:, mine, :, 0], ALU.mult))
                link(dve.tensor_tensor(g[:, mine, :, 1], g[:, mine, :, 1], m[:, mine, :, 1], ALU.add))
                dve.wait_ge(s_xs, 8 * (k + 1))
                dve.tensor_copy(g[:, :, :, 0], m[:, :, :, 0]).then_inc(s_gin, 1)

            def variance(k):
                dve.wait_ge(s_gout, k + 1)
                link(dve.tensor_copy(yd[0][:, 16:32], pf[:, 0:16]))
                link(dve.tensor_tensor(vareps, gout[:, :, :, 0], gout[:, :, :, 0], ALU.mult))
                link(dve.tensor_tensor(vareps, gout[:, :, :, 1], vareps, ALU.subtract))
                dve.tensor_scalar(vareps, vareps, EPS, None, ALU.add).then_inc(s_var, 1)

            def scale(k):
                dve.wait_ge(s_rstd, k + 1)
                dve.wait_ge(s_cw, 16)
                dve.tensor_tensor(gmr.rearrange("p c j -> p j c"), gout[:, :, :, 0], rstd, ALU.mult).then_inc(s_gmr, 1)
                g = gm[:, :, k * BATCH:(k + 1) * BATCH]
                m = mv[:, k * BATCH:(k + 1) * BATCH, :, 0].rearrange("p j c -> p c j")
                link(dve.tensor_tensor(g, m, rstd.rearrange("p j c -> p c j"), ALU.mult))
                dve.wait_ge(s_gmr, k + 1)
                dve.tensor_tensor(g, g, gmr, ALU.subtract).then_inc(s_gm, 1)
                if k >= 2:
                    dve.wait_ge(s_fmm, 2 * (k - 1))
                dve.tensor_tensor(wsc[k % 2], cw[:, :, 0:CM].unsqueeze(2).to_broadcast([128, NC2, BATCH, CM]),
                                  rstd.rearrange("p j c -> p c j").unsqueeze(3).to_broadcast([128, NC2, BATCH, CM]),
                                  ALU.mult).then_inc(s_wsc, 1)

            def f_bias(k):
                dve.wait_ge(s_pbias, k + 1)
                if k >= 2:
                    dve.wait_ge(s_fev, 2 * (k - 1))
                f = fbias[:, 2 * (k % 2):2 * (k % 2) + 2]
                for parts, first in ((LO, 0), (HI, 1)):
                    dve.tensor_scalar(f[parts, :], pf[parts, HALF + first:HALF + 4:2], -1.0, cb[parts, :],
                                      ALU.mult, ALU.add).then_inc(s_fbias, 1)

            def constants():
                dve.wait_ge(s_const, 32)
                dve.tensor_scalar(nwb[:, :], wb, -1.0, None, ALU.mult)
                dve.tensor_scalar(nwbk[:, :], wb, -1.0 / KEYS, None, ALU.mult)
                link(dve.tensor_tensor(fb, fb, wb, ALU.add))
                for kk in range(2):
                    ins = dve.tensor_tensor(kab[:, kk:kk + 1], mixv[:, 3 * kk:3 * kk + 1],
                                            mixv[:, 3 * kk + 1:3 * kk + 2], ALU.add)
                link(ins)
                for kk, (t0, t1) in enumerate(((0, N1), (N1, N1 + N2))):
                    ins = dve.tensor_scalar(dt[:, t0:t1], tapv[:, N1 + N2 + t0:N1 + N2 + t1], kab[:, kk:kk + 1],
                                            mixv[:, 3 * kk + 2:3 * kk + 3], ALU.mult, ALU.add)
                link(ins)

            for k in range(BATCHES):
                if k >= 1:
                    variance(k - 1)
                x_stats(k, 1)
                if k >= 1:
                    scale(k - 1)
                    f_bias(k - 1)
                x_stats(k, 3)
                group_sums(k)
                if k == 0:
                    constants()
            k = BATCHES - 1
            variance(k)
            lo_a(0)
            scale(k)
            f_bias(k)

            dve.wait_ge(s_gmm, 1)
            link(dve.tensor_scalar(gall, pf[:, 64:64 + N], cb, 0.0, ALU.add, ALU.max))
            link(dve.reduce_sum(gsum, gall, AX.X))
            for kk in range(2):
                ins = dve.tensor_scalar(kdom[:, kk:kk + 1], gsum, 1.0 / N, mixv[:, 3 * kk + 1:3 * kk + 2],
                                        ALU.mult, ALU.mult)
            link(ins)
            for kk in range(2):
                dve.tensor_scalar(s12[:, kk, :], gall, mixv[:, 3 * kk:3 * kk + 1], kdom[:, kk:kk + 1],
                                  ALU.mult, ALU.add).then_inc(s_s12, 1)
            dve.wait_ge(s_s12, 2)
            for parts, first in ((LO, 0), (HI, 1)):
                ins = dve.tensor_copy(sd[parts, :, :], s12[parts, :, first::4])
            link(ins)
            gd3 = gd[:, :].rearrange("p (i t) -> p i t", i=BATCHES)
            for kk, (t0, t1) in enumerate(((0, N1), (N1, N1 + N2))):
                ins = dve.tensor_tensor(gd3[:, :, t0:t1],
                                        tapv[:, t0:t1].unsqueeze(1).to_broadcast([128, BATCHES, t1 - t0]),
                                        sd[:, kk, :].unsqueeze(2).to_broadcast([128, BATCHES, t1 - t0]), ALU.mult)
            link(ins)
            link(dve.tensor_tensor(gd3, gd3, dt.unsqueeze(1).to_broadcast([128, BATCHES, N1 + N2]), ALU.add))
            dve.tensor_scalar(gd[:, :], gd[:, :], 0.0, None, ALU.max).then_inc(s_gd, 1)
            dve.tensor_tensor(fb, pf[:, 96:96 + NC2], fb, ALU.add).then_inc(s_fb, 1)
            dve.wait_ge(s_gd, 1)
            base_steps = steps[0]

            PER = NA + 2 * (N2 - 1) - 1

            def taps(i, second, first_pair=False, split_a=False, split_b=False):
                n = [NA if second else 0]

                def chained(ins, back):
                    n[0] += 1
                    ins.then_inc(s_dve, 1)
                    dve.wait_ge(s_dve, i * PER + (base_steps + n[0] - back))

                base = i * PAIR
                acc1 = image(pd[:, :])
                acc2 = image(yd[1][:, :])

                def tap1(t, parts=slice(0, 128), dst=acc1):
                    f, g = shifted(fpad, base, OFFSET[t], parts), gdi[parts, t:t + 1]
                    return dve.scalar_tensor_tensor(out=dst, in0=f, scalar=g, in1=acc1[parts],
                                                    op0=ALU.mult, op1=ALU.add)

                def tap2(j, parts=slice(0, 128), dst=acc2):
                    f, g = shifted(fpad, base, OFFSET[NA + j], parts), gdi[parts, N1 + j:N1 + j + 1]
                    return dve.scalar_tensor_tensor(out=dst, in0=f, scalar=g, in1=acc2[parts],
                                                    op0=ALU.mult, op1=ALU.add)

                if not second:
                    dve.wait_ge(s_yd, START + i * 4)
                    dve.tensor_copy(gdi[:, :], gd[:, bass.ds(i * (N1 + N2), N1 + N2)]).then_inc(s_gdi, 1)
                    dve.wait_ge(s_gdi, i + 1)
                    chained(dve.tensor_scalar(acc1, shifted(fpad, base, OFFSET[0]), gdi[:, 0:1], None, ALU.mult), 0)
                    for t in range(1, NA):
                        chained(tap1(t), 0)
                        if t == 6 and split_b:
                            lo_b(i)
                    return
                dve.wait_ge(s_tap0, i + 1)
                for j in range(N2 - 1):
                    if j:
                        chained(tap2(j), 1)
                    chained(tap1(NA + j), 1)
                    if j == 2 and split_a:
                        lo_a(i + 1)
                assert n[0] == PER
                dve.wait_ge(s_dve, i * PER + (base_steps + PER))
                if not first_pair:
                    dve.wait_ge(s_fuse, START + place("D0", i - 1) + HALVES)
                tap2(N2 - 1, LO, image(yd[0][HI, :])).then_inc(s_yd, 1)
                tap2(N2 - 1, HI, image(yd[1][HI, :])).then_inc(s_yd, 1)
                tap1(N1 - 1, LO, image(yd[0][LO, :])).then_inc(s_yd, 1)
                dve.wait_ge(s_yd, START + i * 4 + 1)
                tap1(N1 - 1, HI, image(yd[1][LO, :])).then_inc(s_yd, 1)

            def inner_blocks(i):
                dve.wait_ge(s_l1e, START + i * 2 + 2)
                for j in range(BATCH):
                    inner_image(dve, i, j).then_inc(s_inner, 1)

            def round_(i, first=False):
                taps(i, True, first_pair=first, split_a=True)
                taps(i + 1, False, split_b=True)
                if not first:
                    inner_blocks(i - 1)

            dve.wait_ge(s_fev, 2 * (BATCHES - 1))
            dve.wait_ge(s_at, 1)
            taps(0, False, split_b=True)
            dve.wait_ge(s_fev, 2 * BATCHES)
            dve.wait_ge(s_gw, 6)
            round_(0, first=True)
            with dve.Fori(1, BATCHES - 1) as i:
                round_(i)
            taps(BATCHES - 1, True)
            b6 = gd[:, 0:48].rearrange("p (j c h s) -> p j c h s", j=2, c=NC2, h=2)
            halves = [(j, c, h) for j in (1, 0) for c in range(NC2) for h in range(2)]
            for n, (j, c, h) in enumerate(halves):
                dve.wait_ge(s_fuse, START + HALVES * (N - 2) + n + 1)
                half = xh(N - BATCH + j, c, h)
                dve.scalar_tensor_tensor(out=half, in0=pf[:, h * HALF:(h + 1) * HALF], scalar=fb[:, c:c + 1],
                                         in1=half, op0=ALU.add, op1=ALU.add).then_inc(s_addl, 1)
                if n:
                    dve.wait_ge(s_addl, n)
                    j, c, h = halves[n - 1]
                    dve.bn_stats(b6[:, j, c, h, :], xh(N - BATCH + j, c, h))
            dve.wait_ge(s_addl, 8)
            steps[0] = base_steps + BATCHES * PER
            link(dve.bn_stats(b6[:, 0, 1, 1, :], xh(N - BATCH, 1, 1)))
            for j in (1, 0):
                for c in range(NC2):
                    ins = dve.bn_aggr(mv[:, N - BATCH + j, c, :], b6[:, j, c, :, :].rearrange("p h s -> p (h s)"))
            link(ins)
            mean, var = (mv[:, N - BATCH:N - BATCH + 2, :, e] for e in range(2))
            col0 = 16 * (BATCHES - 1)
            sums, squares = (accg[:, col0 + o:col0 + o + 4].rearrange("p (j c) -> p j c", c=NC2) for o in (0, 8))
            link(dve.tensor_tensor(mean, mean, wb.unsqueeze(1).to_broadcast([128, 2, NC2]), ALU.subtract))
            link(dve.tensor_tensor(squares, mean, mean, ALU.mult))
            link(dve.tensor_tensor(squares, squares, var, ALU.add))
            dve.tensor_scalar(sums, mean, float(HW), None, ALU.mult).then_inc(s_sums, 1)
            dve.tensor_scalar(squares, squares, float(HW), None, ALU.mult).then_inc(s_sums, 1)
            dve.wait_ge(s_l1e, stored + 2)
            for j in (2, 3):
                inner_image(dve, BATCHES - 2, j).then_inc(s_inner, 1)
            means = acc_w[:, 32 * (BATCHES - 1):32 * (BATCHES - 1) + 4]
            img = image(xs[:, (N - BATCH) * NC2 * HW:((N - BATCH) * NC2 + 1) * HW])
            for w in range(4):
                r, col = 4 + 8 * (w // 2), 4 + 8 * (w % 2)
                ins = dve.reduce_sum(means[:, w:w + 1], img[:, r:r + WIN, col:col + WIN], AX.XY)
            link(ins)
            dve.tensor_scalar(means, means, 1.0 / KEYS, wb[:, 0:1], ALU.mult, ALU.subtract).then_inc(s_sums, 1)
            dve.wait_ge(s_l1e, stored + 5)
            for j in (2, 3):
                inner_image(dve, BATCHES - 1, j).then_inc(s_inner, 1)
            dve.wait_ge(s_l1e, stored + 6)
            inner_image(dve, BATCHES - 1, 0).then_inc(s_inner, 1)

        @block.tensor
        def _(pe):
            pe.sem_inc(s_pass, START)
            pe.sem_inc(s_fuse, START)
            pe.wait_ge(s_const, 32)
            pe.wait_ge(s_cw, 16)

            def groups(k):
                pe.wait_ge(s_gin, k + 1)
                pe.matmul(pf[:, 0:16], gmat, gin[k % 2].rearrange("p j c s -> p (j c s)"),
                          start=True, stop=True).then_inc(s_gout, 1)

            def f_batch(k, between=None):
                pe.wait_ge(s_gmr, k + 1)
                for c in range(NC2):
                    mm = pe.matmul(pf[:, HALF:HALF + 4], cw[:, c, :], gmr[:, c, :], start=(c == 0), stop=(c == NC2 - 1))
                mm.then_inc(s_pbias, 1)
                if k == BATCHES - 1:
                    pe.wait_ge(s_gm, BATCHES)
                    for c in range(NC2):
                        pe.matmul(pf[:, 64:64 + N], cw[:, c, :], gm[:, c, :], start=(c == 0), stop=(c == NC2 - 1))
                    for c in range(NC2):
                        mm = pe.matmul(pf[:, 96 + c:97 + c], fw[:, 128 * c:128 * (c + 1)], yb,
                                       start=True, stop=True)
                    mm.then_inc(s_gmm, 1)
                    pe.wait_ge(s_attw, 32)
                    for c in range(NC2):
                        for e in range(NC2):
                            mm = pe.matmul(pd[:, C * c:C * (c + 1)], wv[:, C * e + 128 * c:C * e + 128 * (c + 1)],
                                           wot[:, C * e:C * (e + 1)], start=(e == 0), stop=(e == NC2 - 1))
                    mm.then_inc(s_atm, 1)
                pe.wait_ge(s_wsc, k + 1)
                for p, dst in enumerate((pu, pv)):
                    if k >= 1:
                        pe.wait_ge(s_fev, 2 * (k - 1) + p + 1)
                    for h in range(2):
                        for c in range(NC2):
                            for m, parts in enumerate((LO, HI)):
                                j = 2 * p + m
                                at = ((k * BATCH + j) * NC2 + c) * HW + h * HALF
                                mm = pe.matmul(dst[parts, h * HALF:(h + 1) * HALF], wsc[k % 2][:, c, j, :],
                                               xs[:, at:at + HALF], start=(c == 0), stop=(c == NC2 - 1))
                    mm.then_inc(s_fmm, 1)
                    if p == 0 and between:
                        between()

            groups(0)
            f_batch(0, lambda: groups(1))
            for k in range(1, BATCHES):
                if k == 2:
                    groups(2)
                f_batch(k, (lambda: groups(3)) if k == 2 else None)

            def chunk(i, m, k):
                q0, n = CHUNKS[k]
                j = m * NCH + k
                if k == 0:
                    pe.wait_ge(s_hl[m], i + 1)
                    pe.wait_ge(s_uev, START + i * 2 + m)
                if q0 == NA:
                    pe.wait_ge(s_vev, START + i * 2 + m)
                pe.wait_ge(s_diag, i * (2 * NCH) + (j + 1))
                dst = pu if q0 < NA else pv
                for q in range(q0, q0 + n):
                    lhs = wdiag[j % 2][:, (q - q0) * 128:(q - q0 + 1) * 128]
                    for h in range(2):
                        rhs = shifted(hl[m], 0, OFFSET[tap_of(q)], rows=slice(16 * h, 16 * h + 16))
                        mm = pe.matmul(dst[:, h * HALF:(h + 1) * HALF], lhs, rhs,
                                       start=(q in (0, NA)), stop=(q in (NA - 1, PASSES - 1)))
                mm.then_inc(s_pass, 1)

            def fuse(what, i, u):
                if u == 0 and what in "ab":
                    done = START + i * 2 + (1 if what == "a" else 2)
                    pe.wait_ge(s_uev, done)
                    pe.wait_ge(s_vev, done)
                if u == 0 and what == "D1":
                    pe.wait_ge(s_yd, START + i * 4 + 4)
                before = place(what, i) + (u - 1)
                if isinstance(before, int) and before > HALVES * (N - 2):
                    pe.wait_ge(s_addl, before - HALVES * (N - 2))
                else:
                    pe.wait_ge(s_tmp, at_least(START, START + before))
                c, h = u // 2, u % 2
                operands = {"D0": ((fw, yd[0]),), "D1": ((fw, yd[1]),)}.get(
                    what, ((fwu, uv[:, 0:HW]), (fw, uv[:, HW:2 * HW])))
                for e, (wt, y) in enumerate(operands):
                    mm = pe.matmul(pf[:, h * HALF:(h + 1) * HALF], wt[:, 128 * c:128 * (c + 1)],
                                   y[:, h * HALF:(h + 1) * HALF], start=(e == 0), stop=(e == len(operands) - 1))
                mm.then_inc(s_fuse, 1)

            def group_product(n, js=ALL, i=None, whole=False):
                cols, i = columns_of(js), n if i is None else i
                size = cols.stop - cols.start
                sums = accg[:, bass.ds(i * 16, 16)].rearrange("p (e m) -> p e m", e=2)[:, :, cols]
                mm = pe.matmul(pu[:, 0:16].rearrange("p (e m) -> p e m", e=2)[:, :, cols], gmat, sums,
                               start=True, stop=whole)
                if not whole:
                    pe.matmul(pu[:, cols], gmat, acc1[:, bass.ds(i * 8 + cols.start, size)], start=False, stop=False)
                    mm = pe.matmul(pu[:, cols], gmat, mvs[:, bass.ds(i * 8 + cols.start, size)], start=False, stop=True)
                mm.then_inc(s_l1g, 1)

            def attention(n, js=ALL, dst=pf[:, 0:32]):
                pe.wait_ge(s_gnw, n + 1)
                first, size = 4 * js.start, 4 * (js.stop - js.start)
                for o in range(NC2):
                    for c in range(NC2):
                        mm = pe.matmul(dst[:, 16 * o + first:16 * o + first + size],
                                       at[:, C * c + 128 * o:C * c + 128 * (o + 1)],
                                       l1[:, 72 + 16 * c + first:72 + 16 * c + first + size],
                                       start=(c == 0), stop=(c == NC2 - 1))
                mm.then_inc(s_vec, 1)

            def slot(chunks, halves, beside=None):
                for n in range(max(len(chunks), 4)):
                    if n < len(chunks):
                        chunk(*chunks[n])
                    if beside:
                        beside(n)
                    if halves and n < 4:
                        fuse(*halves, n)

            def round_(i, first=False, last=False):
                def slot0(n):
                    if not first and n == 0:
                        pe.wait_ge(s_l1e, START + i * 2 - 2)

                def slot3(n):
                    if n == 1:
                        pe.wait_ge(s_stat, stats_before("D0", i - 1) + STATS)
                        pe.wait_ge(s_uev, START + i * 2 + 3)
                        group_product(i - 1)

                slot([(i, 1, k) for k in range(UCH)], ("a", i), slot0)
                slot([(i, 1, k) for k in range(UCH, NCH)], None if first else ("D0", i - 1))
                slot([] if last else [(i + 1, 0, k) for k in range(UCH)], ("b", i))
                if last:
                    return
                slot([(i + 1, 0, k) for k in range(UCH, NCH)], ("D1", i), None if first else slot3)
                if not first:
                    pe.wait_ge(s_tmp, START + place("D1", i) + 3)
                    attention(i - 1)

            pe.wait_ge(s_fev, 2 * BATCHES - 1)
            slot([(0, 0, k) for k in range(UCH)], None)
            pe.wait_ge(s_fev, 2 * BATCHES)
            pe.wait_ge(s_at, 1)
            pe.wait_ge(s_fb, 1)
            slot([(0, 0, k) for k in range(UCH, NCH)], None)
            round_(0, first=True)
            with pe.Fori(1, BATCHES - 1) as i:
                round_(i)
            round_(BATCHES - 1, last=True)
            fuse("D1", BATCHES - 1, 0)
            fuse("D1", BATCHES - 1, 1)
            pe.wait_ge(s_stat, STATS * (N - 3) - 2)
            pe.wait_ge(s_uev, START + 2 * BATCHES)
            group_product(BATCHES - 2)
            fuse("D1", BATCHES - 1, 2)
            fuse("D1", BATCHES - 1, 3)
            fuse("D0", BATCHES - 1, 0)
            attention(BATCHES - 2, dst=pu[:, HALF:HALF + 32])
            for u in range(1, 4):
                fuse("D0", BATCHES - 1, u)
            pe.wait_ge(s_stat, STATS * (N - 2))
            group_product(last_p, PAIR_P)
            pe.wait_ge(s_sums, 2)
            pe.wait_ge(s_l1e, stored + 3)
            group_product(last_d, PAIR_D, BATCHES - 1, whole=True)
            attention(last_p, PAIR_P, pu[:, HALF:HALF + 32])
            pe.wait_ge(s_l1e, stored + 5)
            attention(last_d, PAIR_D, pu[:, HALF:HALF + 32])


def kernel(**inputs):
    import concourse.bacc as bacc
    from concourse.bass_utils import run_bass_kernel_spmd as run

    a = {k: np.ascontiguousarray(v) for k, v in inputs.items()}
    k1, k2 = a["L0_conv_conv_kernel_w"].reshape(-1)[TAPS], a["L0_conv_conv_kernel2_w"].reshape(-1)
    b1, b2 = a["L0_conv_conv_kernel_b"][TAPS], a["L0_conv_conv_kernel2_b"]
    channel = np.arange(128)
    group_mean = (channel[:, None] // GROUP == channel[None, :] // GROUP).astype(np.float32) / GROUP
    ident = (channel[:, None] % CM == np.arange(CM)[None, :]).astype(np.float32)
    cw_t = a["L0_conv_conv_w"].reshape(CM, C).T
    fw_t = a["L0_conv_fuse_w"].reshape(C, 2 * CM).T
    conv_b = a["L0_conv_conv_b"].reshape(CM, 1)
    y_bias = np.concatenate([a["L0_conv_adap_bias"], a["L0_conv_atrous_bias"]]).reshape(2 * CM, 1)
    fuse_b = a["L0_conv_fuse_b"].reshape(NC2, 128).T
    wout_b = a["L1_conv_Wout_b"].reshape(NC2, 128).T
    arrays = {
        "x": a["x"],
        "cw_t": np.concatenate([cw_t, cw_t], 1),
        "taps": np.concatenate([k1, k2, b1, b2, a["L0_conv_conv_k_w"].reshape(-1), a["L0_conv_conv_k_b"],
                                a["L0_conv_conv_k2_w"].reshape(-1), a["L0_conv_conv_k2_b"]]).reshape(1, -1),
        "columns": np.concatenate([group_mean, ident, fw_t, np.concatenate([fw_t[:CM], fw_t[:CM]], 0),
                                   np.concatenate([conv_b, conv_b], 0), y_bias, fuse_b, wout_b], 1),
        "wkv": a["L1_conv_Wkv"],
        "wout_t": a["L1_conv_Wout_w"].T,
    }
    arrays = {k + "_dram": np.ascontiguousarray(v) for k, v in arrays.items()}
    nc = bacc.Bacc("TRN2", target_bir_lowering=False, num_devices=1)
    args = [nc.dram_tensor(k, v.shape, mybir.dt.from_np(v.dtype), kind="ExternalInput").ap()
            for k, v in arrays.items()]
    out = nc.dram_tensor("out_dram", (N, C, H, W), F32, kind="ExternalOutput").ap()
    build(nc, *args, out)
    return run(nc, [arrays], core_ids=[0]).results[0]["out_dram"]
```
